# Optimizing a Trainium2 kernel written in Bass

```python
import numpy as np
import jax
import jax.numpy as jnp

def _softmax(x, axis=-1):
    return jax.nn.softmax(x, axis=axis)

def _gelu(x):
    return jax.nn.gelu(x, approximate=True)

def _silu(x):
    return jax.nn.silu(x)

def _sigmoid(x):
    return jax.nn.sigmoid(x)

def _layernorm(x, axis=-1, eps=1e-05):
    m = jnp.mean(x, axis=axis, keepdims=True)
    v = jnp.var(x, axis=axis, keepdims=True)
    return (x - m) / jnp.sqrt(v + eps)

def _scatter_add(tgt, idx, src, axis=0):
    return tgt.at[idx].add(src)

def _segment_sum(src, seg, n):
    return jax.ops.segment_sum(src, seg, n)
kernel_name = 'mk_flamingo_gated_d2_seqx_r8_e60e9b'

def setup_inputs(seed: int=0):
    np.random.seed(seed)
    _w = jnp.asarray

    def _rec_inputs():
        import jax
        import jax.numpy as jnp
        _rk = jax.random.key(seed)
        x = -0.0002928 + 1 * jax.random.normal(jax.random.fold_in(_rk, 1), (16, 56, 128), jnp.float32)
        _lenS = 56 - jax.random.randint(jax.random.fold_in(_rk, 7), (16,), 0, max(1, 56 // 4) + 1, jnp.int32)
        _lenS2 = 1500 - jax.random.randint(jax.random.fold_in(_rk, 8), (16,), 0, max(1, 1500 // 4) + 1, jnp.int32)
        _ctx_1024P = jax.random.normal(jax.random.fold_in(_rk, 11), (16, 16, 128), jnp.float32)
        _ctx_1024c = jax.random.dirichlet(jax.random.fold_in(_rk, 511), 0.3 * jnp.ones((16,), jnp.float32), (16, 1500))
        _ctx_1024t = jnp.einsum('bsk,bkd->bsd', _ctx_1024c, _ctx_1024P)
        _ctx_1024t = _ctx_1024t * jax.lax.rsqrt(jnp.mean(jnp.square(_ctx_1024t)) + 1e-12) * 0.953939
        ctx_1024 = -1.39393e-06 + 0.999914 * (_ctx_1024t + 0.3 * jax.random.normal(jax.random.fold_in(_rk, 611), (16, 1500, 128), jnp.float32))
        _validS = jnp.arange(56)[None, :] < _lenS[:, None]
        _validS2 = jnp.arange(1500)[None, :] < _lenS2[:, None]
        _causal = jnp.tril(jnp.ones((56, 56), dtype=bool))
        mask_1x1xSxS2_ik0 = jnp.where(jnp.broadcast_to(_validS2[0:1, None, None, :], (1, 1, 56, 1500)), 0, 1).astype(jnp.int32)
        _g = jax.random.normal(jax.random.fold_in(_rk, 9001), (2, 2), jnp.float32)
        _g = jnp.sign(_g) * jnp.maximum(jnp.abs(_g), 1.0) + (_g == 0) * 1.0
        g_xattn = _g[0]
        g_ffn = _g[1]
        return (x, ctx_1024, mask_1x1xSxS2_ik0, g_xattn, g_ffn)
    x, ctx_1024, mask_1x1xSxS2_ik0, g_xattn, g_ffn = _rec_inputs()

    def _L0_xattn_setup():
        import jax, jax.numpy as jnp
        import numpy as np
        B, T, C = (2, 256, 128)
        NUM_HEADS, QK_LEN, V_LEN = (16, 64, 64)

        def _split_heads(x, n_heads, d):
            b, t, _ = x.shape
            return x.reshape(b, t, n_heads, d).transpose(0, 2, 1, 3)
        key = jax.random.key(seed)
        ks = jax.random.split(key, 11)
        s = 0.02
        return {'Q': jax.random.normal(ks[0], (B, T, C), jnp.float32), 'K': jax.random.normal(ks[1], (B, T, C), jnp.float32), 'V': jax.random.normal(ks[2], (B, T, C), jnp.float32), 'Wq': jax.random.normal(ks[3], (C, NUM_HEADS * QK_LEN), jnp.float32) * s, 'bq': jnp.zeros((NUM_HEADS * QK_LEN,), jnp.float32), 'Wk': jax.random.normal(ks[4], (C, NUM_HEADS * QK_LEN), jnp.float32) * s, 'bk': jnp.zeros((NUM_HEADS * QK_LEN,), jnp.float32), 'Wv': jax.random.normal(ks[5], (C, NUM_HEADS * V_LEN), jnp.float32) * s, 'bv': jnp.zeros((NUM_HEADS * V_LEN,), jnp.float32), 'Wo': jax.random.normal(ks[6], (NUM_HEADS * V_LEN, C), jnp.float32) * s, 'bo': jnp.zeros((C,), jnp.float32)}
    _L0_xattn_all = _L0_xattn_setup()
    _L0_xattn_in = {k: v for k, v in _L0_xattn_all.items() if k in ('Wq', 'bq', 'Wk', 'bk', 'Wv', 'bv', 'Wo', 'bo')}
    del _L0_xattn_all

    def _L0_ffn_setup():
        import jax, jax.numpy as jnp
        import numpy as np
        B, L, H, E, FF, C = (4, 256, 128, 8, 512, 2)
        key = jax.random.key(seed)
        ks = jax.random.split(key, 6)
        s = 0.02
        return {'x': jax.random.normal(ks[0], (B, L, H), dtype=jnp.float32), 'Wg': jax.random.normal(ks[1], (H, E), dtype=jnp.float32) * s, 'W1': jax.random.normal(ks[2], (E, H, FF), dtype=jnp.float32) * s, 'b1': jnp.zeros((E, FF), dtype=jnp.float32), 'W2': jax.random.normal(ks[3], (E, FF, H), dtype=jnp.float32) * s, 'b2': jnp.zeros((E, H), dtype=jnp.float32)}
    _L0_ffn_all = _L0_ffn_setup()
    _L0_ffn_in = {k: v for k, v in _L0_ffn_all.items() if k in ('Wg', 'W1', 'b1', 'W2', 'b2')}
    del _L0_ffn_all

    def _L1_xattn_setup():
        import jax, jax.numpy as jnp
        import numpy as np
        D_MODEL = 128
        H = 16
        D_K = D_MODEL // H
        NEG = -1000000000.0
        key = jax.random.key(seed)
        ks = jax.random.split(key, 7)
        B, S = (4, 256)
        q = jax.random.normal(ks[0], (B, S, D_MODEL), dtype=jnp.float32)
        k = jax.random.normal(ks[1], (B, S, D_MODEL), dtype=jnp.float32)
        v = jax.random.normal(ks[2], (B, S, D_MODEL), dtype=jnp.float32)
        mask = jnp.tril(jnp.ones((S, S), dtype=jnp.int32))[None, None, :, :]
        scale = 0.02
        w_q = jax.random.normal(ks[3], (D_MODEL, D_MODEL), dtype=jnp.float32) * scale
        w_k = jax.random.normal(ks[4], (D_MODEL, D_MODEL), dtype=jnp.float32) * scale
        w_v = jax.random.normal(ks[5], (D_MODEL, D_MODEL), dtype=jnp.float32) * scale
        w_o = jax.random.normal(ks[6], (D_MODEL, D_MODEL), dtype=jnp.float32) * scale
        return {'q': q, 'k': k, 'v': v, 'mask': mask, 'w_q': w_q, 'w_k': w_k, 'w_v': w_v, 'w_o': w_o}
    _L1_xattn_all = _L1_xattn_setup()
    _L1_xattn_in = {k: v for k, v in _L1_xattn_all.items() if k in ('w_q', 'w_k', 'w_v', 'w_o')}
    del _L1_xattn_all

    def _L1_ffn_setup():
        import jax, jax.numpy as jnp
        import numpy as np
        B, T, C = (4, 256, 128)
        E, F, K = (8, 256, 2)
        key = jax.random.key(seed)
        k0, k1, k2, k3 = jax.random.split(key, 4)
        s = lambda d: 1.0 / np.sqrt(d)
        x = jax.random.normal(k0, (B, T, C), dtype=jnp.float32)
        Wr = jax.random.normal(k1, (E, C), dtype=jnp.float32) * s(C)
        W1 = jax.random.normal(k2, (E, 2 * F, C), dtype=jnp.float32) * s(C)
        W2 = jax.random.normal(k3, (E, C, F), dtype=jnp.float32) * s(F)
        return {'x': x, 'Wr': Wr, 'W1': W1, 'W2': W2}
    _L1_ffn_all = _L1_ffn_setup()
    _L1_ffn_in = {k: v for k, v in _L1_ffn_all.items() if k in ('Wr', 'W1', 'W2')}
    del _L1_ffn_all
    return {'x': x, 'ctx_1024': ctx_1024, 'mask_1x1xSxS2_ik0': mask_1x1xSxS2_ik0, 'g_xattn': g_xattn, 'g_ffn': g_ffn, 'L0_xattn_Wq': _L0_xattn_in['Wq'], 'L0_xattn_bq': _L0_xattn_in['bq'], 'L0_xattn_Wk': _L0_xattn_in['Wk'], 'L0_xattn_bk': _L0_xattn_in['bk'], 'L0_xattn_Wv': _L0_xattn_in['Wv'], 'L0_xattn_bv': _L0_xattn_in['bv'], 'L0_xattn_Wo': _L0_xattn_in['Wo'], 'L0_xattn_bo': _L0_xattn_in['bo'], 'L0_ffn_Wg': _L0_ffn_in['Wg'], 'L0_ffn_W1': _L0_ffn_in['W1'], 'L0_ffn_b1': _L0_ffn_in['b1'], 'L0_ffn_W2': _L0_ffn_in['W2'], 'L0_ffn_b2': _L0_ffn_in['b2'], 'L1_xattn_w_q': _L1_xattn_in['w_q'], 'L1_xattn_w_k': _L1_xattn_in['w_k'], 'L1_xattn_w_v': _L1_xattn_in['w_v'], 'L1_xattn_w_o': _L1_xattn_in['w_o'], 'L1_ffn_Wr': _L1_ffn_in['Wr'], 'L1_ffn_W1': _L1_ffn_in['W1'], 'L1_ffn_W2': _L1_ffn_in['W2']}

def reference(x, ctx_1024, mask_1x1xSxS2_ik0, g_xattn, g_ffn, L0_xattn_Wq, L0_xattn_bq, L0_xattn_Wk, L0_xattn_bk, L0_xattn_Wv, L0_xattn_bv, L0_xattn_Wo, L0_xattn_bo, L0_ffn_Wg, L0_ffn_W1, L0_ffn_b1, L0_ffn_W2, L0_ffn_b2, L1_xattn_w_q, L1_xattn_w_k, L1_xattn_w_v, L1_xattn_w_o, L1_ffn_Wr, L1_ffn_W1, L1_ffn_W2):
    import jax
    import jax.numpy as jnp

    def _L0_xattn_ref(Q, K, V, Wq, bq, Wk, bk, Wv, bv, Wo, bo):
        import jax, jax.numpy as jnp
        import numpy as np
        B, T, C = (2, 256, 128)
        NUM_HEADS, QK_LEN, V_LEN = (16, 64, 64)

        def _split_heads(x, n_heads, d):
            b, t, _ = x.shape
            return x.reshape(b, t, n_heads, d).transpose(0, 2, 1, 3)
        q = _split_heads(Q @ Wq + bq, NUM_HEADS, QK_LEN)
        k = _split_heads(K @ Wk + bk, NUM_HEADS, QK_LEN)
        v = _split_heads(V @ Wv + bv, NUM_HEADS, V_LEN)
        scale = 1.0 / jnp.sqrt(jnp.asarray(QK_LEN, q.dtype))
        scores = jnp.einsum('bhqd,bhkd->bhqk', q, k) * scale
        attn = jax.nn.softmax(scores, axis=-1)
        out = jnp.einsum('bhqk,bhkd->bhqd', attn, v)
        out = out.transpose(0, 2, 1, 3).reshape(Q.shape[0], Q.shape[1], NUM_HEADS * V_LEN)
        return out @ Wo + bo

    def _L0_ffn_ref(x, Wg, W1, b1, W2, b2):
        import jax, jax.numpy as jnp
        import numpy as np
        B, L, H, E, FF, C = (4, 256, 128, 8, 512, 2)
        b, l, h = x.shape
        e = Wg.shape[1]
        n = b * l
        k = min(max(int(n * C / e), 1), n)
        xt = x.reshape(n, h)
        S = jax.nn.sigmoid(xt @ Wg).T
        G, I = jax.lax.top_k(S, k)
        ex = xt[I]
        hid = jax.nn.gelu(jnp.einsum('ekh,ehf->ekf', ex, W1) + b1[:, None, :], approximate=False)
        out = (jnp.einsum('ekf,efh->ekh', hid, W2) + b2[:, None, :]) * G[..., None]
        new_x = jnp.zeros_like(xt).at[I.reshape(-1)].add(out.reshape(-1, h))
        return new_x.reshape(b, l, h)

    def _L1_xattn_ref(q, k, v, mask, w_q, w_k, w_v, w_o):
        import jax, jax.numpy as jnp
        import numpy as np
        D_MODEL = 128
        H = 16
        D_K = D_MODEL // H
        NEG = -1000000000.0
        B, S, _ = q.shape

        def proj(x, w):
            return (x @ w.T).reshape(B, -1, H, D_K).transpose(0, 2, 1, 3)
        query = proj(q, w_q)
        key_ = proj(k, w_k)
        value = proj(v, w_v)
        scores = jnp.einsum('bhqd,bhkd->bhqk', query, key_) / jnp.sqrt(jnp.asarray(D_K, dtype=query.dtype))
        scores = jnp.where(mask == 0, jnp.asarray(NEG, dtype=scores.dtype), scores)
        attn = jax.nn.softmax(scores, axis=-1)
        out = jnp.einsum('bhqk,bhkd->bhqd', attn, value)
        out = out.transpose(0, 2, 1, 3).reshape(B, -1, H * D_K)
        return out @ w_o.T

    def _L1_ffn_ref(x, Wr, W1, W2):
        import jax, jax.numpy as jnp
        import numpy as np
        B, T, C = (4, 256, 128)
        E, F, K = (8, 256, 2)
        Bb, Tt, Cc = x.shape
        flat = x.reshape(-1, Cc)
        N = flat.shape[0]
        logits = flat @ Wr.T
        weights, ids = jax.lax.top_k(logits, K)
        weights = jax.nn.softmax(weights, axis=-1)
        rows = jnp.arange(N)[:, None]
        router_weights = jnp.zeros((N, E), dtype=flat.dtype).at[rows, ids].add(weights)
        h = jnp.einsum('nc,efc->nef', flat, W1)
        val, gate = (h[..., :F], h[..., F:])
        act = val * jax.nn.silu(gate)
        expert_outputs = jnp.einsum('nef,ecf->nec', act, W2)
        out = jnp.einsum('nec,ne->nc', expert_outputs, router_weights)
        return out.reshape(Bb, Tt, Cc)
    x = x + jnp.tanh(g_xattn[0]) * _L0_xattn_ref(_layernorm(x, axis=-1), ctx_1024, ctx_1024, L0_xattn_Wq, L0_xattn_bq, L0_xattn_Wk, L0_xattn_bk, L0_xattn_Wv, L0_xattn_bv, L0_xattn_Wo, L0_xattn_bo)
    x = x + jnp.tanh(g_ffn[0]) * _L0_ffn_ref(_layernorm(x, axis=-1), L0_ffn_Wg, L0_ffn_W1, L0_ffn_b1, L0_ffn_W2, L0_ffn_b2)
    x = x + jnp.tanh(g_xattn[1]) * _L1_xattn_ref(_layernorm(x, axis=-1), ctx_1024, ctx_1024, mask_1x1xSxS2_ik0, L1_xattn_w_q, L1_xattn_w_k, L1_xattn_w_v, L1_xattn_w_o)
    x = x + jnp.tanh(g_ffn[1]) * _L1_ffn_ref(_layernorm(x, axis=-1), L1_ffn_Wr, L1_ffn_W1, L1_ffn_W2)
    return x

_drawn_inputs = setup_inputs


def setup_inputs(seed=0):
    import zlib

    import numpy as np

    out = dict(_drawn_inputs(seed))
    spreads = {'g_ffn': (-1.0, 0.573),
     'L0_xattn_bq': (0.0, 0.8),
     'L0_xattn_bk': (0.0, 0.8),
     'L0_xattn_bv': (0.0, 0.1),
     'L0_xattn_bo': (0.0, 0.1),
     'L0_ffn_b1': (0.0, 0.1),
     'L0_ffn_b2': (0.0, 0.1)}
    factors = {'L0_xattn_Wq': 5.528, 'L0_xattn_Wk': 6.29, 'L1_xattn_w_q': 7.827, 'L1_xattn_w_k': 4.578}
    for name, (base, spread) in spreads.items():
        noise = np.random.default_rng([zlib.crc32(name.encode()), seed]).standard_normal(out[name].shape)
        drawn = base * np.exp(spread * noise) if base else spread * noise
        out[name] = jnp.asarray(drawn.astype(out[name].dtype))
    for name, factor in factors.items():
        out[name] = (out[name] * factor).astype(out[name].dtype)
    return out
```

```python
import concourse.bass as bass
from concourse import mybir
from contextlib import ExitStack

F32 = mybir.dt.float32
BF16 = mybir.dt.bfloat16
I32 = mybir.dt.int32
ALU = mybir.AluOpType
ACT = mybir.ActivationFunctionType
AX = mybir.AxisListType.X

P = 128
NB, NQ, C = 16, 56, 128
NK = 1500
KC, KP = 12, 125
H = 16
TOK = NB * NQ
HALF = TOK // 2
TILES = H * NQ // P
STEPS = NB * TILES
PAIR = 2 * TILES
BANKK = 500
DH0, DH1 = 64, 8
E = 8
FF0, FF1 = 512, 256
TOPK = TOK * 2 // E
EPS = 1e-5
MASKED = -float(2 ** 100)
SHIFTS = [27, 23, 19, 15, 11, 7, 3, 0]


def least(eng, sem, value):
    if isinstance(value, int) and value <= 0:
        return
    eng.wait_ge(sem, value)


def apart(eng, done):
    eng.wait_ge(done, 1)


def first_loop_last(eng, count, body):
    body(0)
    with eng.Fori(1, count - 1) as i:
        body(i)
    body(count - 1)


def flamingo(nc, x, ctx_d, mask_d, g_xattn, g_ffn, Wq, bq, Wk, bk, Wv, bv, Wo, bo,
             Wg, W1, b1, W2, b2, w_q, w_k, w_v, w_o, Wr, V1, V2, out):
    stack = ExitStack()
    with stack:
        def sb(name, shape, dt=F32):
            return stack.enter_context(nc.sbuf_tensor(name, shape, dt))

        sems = {}

        def sem(name):
            if name not in sems:
                sems[name] = stack.enter_context(nc.semaphore(name))
            return sems[name]

        xT = sb("xT", [P, TOK])
        xn = sb("xn", [P, TOK])
        sq = sb("sq", [P, TOK])
        xn_s = sb("xn_split", [P, 2, TOK], BF16)
        qo = sb("queries_outputs", [P, 2, H * TOK], BF16)
        W1s = sb("W1_split", [P, 2, E * FF0], BF16)
        W2s = sb("W2_split", [P, 2, E * FF0], BF16)
        V1s = sb("V1_split", [P, 2, E * 2 * FF1], BF16)
        V2s = sb("V2_split", [P, 2, E * FF1], BF16)
        Ms = sb("M_split", [P, 2, H * C], BF16)
        Ns = sb("N_split", [P, 2, H * C], BF16)
        cx = sb("context", [KP, 2, KC * C])
        cT = sb("context_T_split", [C, 2, 2, NK], BF16)
        pr = sb("probs", [P, 2, NK])
        pT = sb("probs_T", [KP, KC * P])
        o_n = sb("outputs_scaled", [P, 2, C])
        ident = sb("ident", [P, P])
        mean_w = sb("mean_w", [P, P])
        block1 = sb("block_ones", [P, P])
        tril = sb("tril", [P, E, E])
        headm = sb("head_mask", [P, H])
        rep = sb("repeat_ident", [NQ, H * NQ], BF16)
        mbias = sb("mask_bias", [NQ, NK], BF16)
        stage = sb("stage", [P, 2, FF0])
        wl1 = sb("L1_proj", [P, 4, C])
        woT = sb("woT", [P, C])
        bias_c = sb("bias_columns", [P, 64])
        U = sb("U", [P, H])
        qbias = sb("qbias", [P, 2, H])
        prod = sb("bq_bk", [P, H])
        rrow = sq[0:H, :]
        rtile = sb("rtile", [STEPS, P])
        rcol = sb("rcol", [P, STEPS])
        crow = sb("crow", [H, 1])
        mx = sb("mx", [P, 4])
        nb = sb("nb", [P, 2])
        sums = sb("sums", [P, 2, 3])
        den = sb("den", [P, 2])
        gates = sb("gates", [P, 4])
        eps_c = sb("eps", [P, 1])
        ones_c = sb("ones_c", [P, 1])
        Wg_rep = sb("Wg_rep", [P, E, 16])
        Wr_T = sb("Wr_T", [P, E])
        wg_raw = sb("Wg_raw", [P, E])
        b1c = sb("b1c", [P, E * 4 + 4])
        b1_now = sb("b1_now", [P, 8])
        b2c = sb("b2c", [P, E])
        pj = sb("pj", [P, 16], I32)
        jsh = sb("jsh", [P, 8], I32)
        powc = sb("powc", [P, 8])
        valid = sb("valid", [P, 8])
        prefix = sb("prefix", [P, 1], I32)
        cand = sb("cand", [P, 1], I32)
        digit = sb("digit", [P, 2])
        digit_i = sb("digit_i", [P, 1], I32)
        flag = sb("flag", [P, 2])
        cols = sb("cols", [P, 8])

        q32 = qo[:, :, :].rearrange("p a n -> p (a n)").bitcast(F32)
        raw = {}
        at = 0
        for name, n in (("Wq", 1024), ("Wk", 1024), ("Wv", 1024), ("Wo", 1024), ("V1", 4096), ("V2", 2048), ("x", 896)):
            raw[name] = q32[:, at:at + n]
            at += n
        pr32 = pr[:, :, :].rearrange("p a n -> p (a n)")
        WqT = pr32[:, 0:1024].rearrange("p (j c) -> p j c", c=C)
        WkT = pr32[:, 1024:2048].rearrange("p (j c) -> p j c", c=C)
        WvT = stage[:, :, :].rearrange("p a n -> p (a n)").rearrange("p (j c) -> p j c", c=C)
        y_e = q32[:, 0:E * TOK]
        scr = q32[:, E * TOK:2 * E * TOK]
        hid = scr[:, 0:1792].rearrange("p (r n) -> p r n", r=4)
        hid_s = scr[:, 1792:3584].bitcast(BF16).rearrange("p (a r n) -> p a r n", a=2, r=4)
        sig = scr[:, 3584:4480]
        tmp = scr[:, 4480:5376]
        sel = scr[:, 5376:6272]
        acc = scr[:, 6272:7168]
        wk_m = q32[:, 0:2048]
        wo_m = q32[:, 2048:4096]
        mask_i = pr32[0:NQ, 0:NK].bitcast(I32)

        r_dram = nc.dram_tensor("r_rows", [NB, H, NQ], F32, kind="Internal").ap()

        ps = stack.enter_context(nc.psum_tensor("ps", [P, 8 * 512], F32))

        def bank(k, n=512, p=P):
            return ps[0:p, k * 512:k * 512 + n]

        block = stack.enter_context(nc.Block())

        def fold_part(dst, a, g):
            v = dst[:, a, :].rearrange("p (a c s n) -> p a c s n", a=2, s=2, n=C)
            return v[:, g % 4 // 2, :, g % 2, :]

        BQ, BK, BV, BO, OB = 0, 8, 16, 24, 25

        def blocks_of(name, n, width=P):
            return [raw[name][:, width * k:width * (k + 1)] for k in range(n)]

        groups = []
        for g in range(2):
            n = 4 - g
            groups.append(("ld_x", blocks_of("x", 7)[4 * g:4 * g + n], P, xT[:, 512 * g:512 * g + P * n], None, 0))
        for name, dst in (("Wq", WqT), ("Wk", WkT), ("Wv", WvT)):
            for g in range(2):
                groups.append((f"ld_{name}", blocks_of(name, 8)[4 * g:4 * g + 4], P,
                               dst[:, 4 * g:4 * g + 4, :], None, 0))
        for g in range(E):
            groups.append(("ld_V1", blocks_of("V1", 32)[4 * g:4 * g + 4], P, None, V1s, 512 * g))
        for g in range(4):
            groups.append(("ld_V2", blocks_of("V2", 16)[4 * g:4 * g + 4], P, None, V2s, 512 * g))
        for g in range(3):
            groups.append(("ld_cx", [cx[:, 0, C * k:C * (k + 1)] for k in range(4 * g, 4 * g + 4)], KP,
                           None, cT[:, 0, :, :], BANKK * g))
        NG = len(groups)
        split_before = [sum(g[4] is not None for g in groups[:k]) for k in range(NG + 1)]

        def context_load(sp, b, parity, want):
            sp.dma_start(cx[:, parity, :], ctx_d[b].rearrange("(p c) d -> p (c d)", c=KC)).then_inc(sem("ld_cx"), 16)

        @block.sync
        def _(sp):
            sp.dma_start(raw["x"].rearrange("p (t c) -> p t c", c=C),
                         x.rearrange("b q c -> (b q) c").rearrange("(t p) c -> p t c", p=P)).then_inc(sem("ld_x"), 16)
            for name, w in (("Wq", Wq), ("Wk", Wk), ("Wv", Wv)):
                sp.dma_start(raw[name], w).then_inc(sem(f"ld_{name}"), 16)
            sp.dma_start(raw["Wo"].rearrange("p (j c) -> p j c", c=C),
                         Wo.rearrange("(j p) c -> p j c", p=P)).then_inc(sem("ld_Wo"), 16)
            sp.dma_start(raw["V1"].rearrange("p (k c) -> p k c", c=C),
                         V1.rearrange("e (k p) c -> p (e k) c", p=P)).then_inc(sem("ld_V1"), 16)
            sp.dma_start(raw["V2"].rearrange("p (e f) -> p e f", e=E),
                         V2.rearrange("e c f -> c e f")).then_inc(sem("ld_V2"), 16)
            context_load(sp, 0, 0, 0)
            for k, w in enumerate((w_q, w_k, w_v, w_o)):
                sp.dma_start(wl1[:, k, :], w).then_inc(sem("ld_l1"), 16)
            sp.wait_ge(sem("r_rows"), 2)
            sp.dma_start(r_dram.rearrange("b h q -> h b q"),
                         rrow.rearrange("h (b q) -> h b q", q=NQ)).then_inc(sem("r_out"), 16)
            sp.wait_ge(sem("r_out"), 16)
            sp.dma_start(rtile[:, :], r_dram.rearrange("b h q -> (b h q)").rearrange("(t p) -> t p", p=P)
                         ).then_inc(sem("r_in"), 16)
            for L in range(2):
                def pair(i):
                    for m in range(2):
                        if L == 1 and m == 1 and isinstance(i, int) and i == NB // 2 - 1:
                            return
                        if isinstance(i, int) and i == 0 and m == 0:
                            if L == 1:
                                sp.wait_ge(sem("a0_O"), STEPS)
                        else:
                            sp.wait_ge(sem(f"a{L}_O"), PAIR * i + TILES * m)
                        if isinstance(i, int):
                            b = (2 * i + m + 1) % NB
                        else:
                            b = 2 * i + (m + 1)
                        context_load(sp, b, (m + 1) % 2, 0)
                first_loop_last(sp, NB // 2, pair)
                if L == 0:
                    sp.wait_ge(sem("a0_T"), 3 * STEPS)
                    sp.dma_start(mask_i, mask_d[0, 0]).then_inc(sem("ld_mask"), 16)
            sp.wait_ge(sem("out_rows"), 2)
            sp.dma_start(out.rearrange("b q c -> (b q) c").rearrange("(t p) c -> p t c", p=P),
                         xn[:, :].rearrange("p (t c) -> p t c", c=C)).then_inc(sem("stored"), 16)
            sp.wait_ge(sem("stored"), 16)

        @block.gpsimd
        def _(pool):
            chain = [0]

            def link(ins):
                chain[0] += 1
                ins.then_inc(sem("pool_chain"), 1)
                pool.wait_ge(sem("pool_chain"), chain[0])

            def small(dst, src, name="ld_small"):
                pool.dma_start(dst, src).then_inc(sem(name), 16)

            pool.memset(b1c[:, E * 4:], 0.0).then_inc(sem("b1_pad"), 1)
            link(pool.memset(bias_c[:, :], 0.0))
            with nc.allow_non_contiguous_dma("a few small columns"):
                for c0, b_ in ((BQ, bq), (BK, bk), (BV, bv)):
                    small(bias_c[:, c0:c0 + 8], b_.rearrange("(j p) -> p j", p=P))
                small(bias_c[:, BO:BO + 1], bo.rearrange("(p a) -> p a", a=1))
                small(gates[:, 0:2], g_xattn.rearrange("(a n) -> a n", a=1).broadcast_to([P, 2]))
                small(gates[:, 2:4], g_ffn.rearrange("(a n) -> a n", a=1).broadcast_to([P, 2]))
                small(wg_raw[:, :], Wg)
                small(Wr_T[:, :], Wr.rearrange("e c -> c e"))
                small(b1c[:, 0:E * 4], b1.rearrange("e (k p) -> p (e k)", p=P))
                small(b2c[:, :], b2.rearrange("e c -> c e"))
            link(pool.memset(ident[:, :], 0.0))
            pool.affine_select(out=ident[:, :], in_=ident[:, :], compare_op=ALU.not_equal, fill=1.0, base=0,
                               pattern=[[-1, P]], channel_multiplier=1).then_inc(sem("ident"), 1)
            pool.memset(mean_w[:, :], 1.0 / C)
            pool.memset(eps_c[:, :], EPS)
            pool.memset(ones_c[:, :], 1.0)
            link(pool.memset(qbias[:, 1, :], 0.0))
            link(pool.memset(prod[:, :], 0.0))
            pool.memset(headm[:, :], 1.0)
            pool.memset(tril[:, :, :], 1.0)
            link(pool.memset(block1[:, :], 1.0))
            link(pool.memset(rep[:, :], 0.0))
            blk = block1[:, :].rearrange("p (b j) -> p b j", j=16)
            link(pool.affine_select(out=blk, in_=blk, compare_op=ALU.is_ge, fill=0.0, base=0,
                                    pattern=[[-16, 8], [0, 16]], channel_multiplier=1))
            link(pool.affine_select(out=blk, in_=blk, compare_op=ALU.is_ge, fill=0.0, base=15,
                                    pattern=[[16, 8], [0, 16]], channel_multiplier=-1))
            link(pool.affine_select(out=headm[:, :], in_=headm[:, :], compare_op=ALU.is_ge, fill=0.0, base=0,
                                    pattern=[[-8, H]], channel_multiplier=1))
            link(pool.affine_select(out=headm[:, :], in_=headm[:, :], compare_op=ALU.is_ge, fill=0.0, base=7,
                                    pattern=[[8, H]], channel_multiplier=-1))
            link(pool.affine_select(out=tril[:, :, :], in_=tril[:, :, :], compare_op=ALU.is_ge, fill=0.0, base=-1,
                                    pattern=[[1, E], [-1, E]], channel_multiplier=0))
            rep3 = rep[:, :].rearrange("j (h q) -> j h q", q=NQ)
            link(pool.affine_select(out=rep3, in_=rep3, compare_op=ALU.not_equal, fill=1.0, base=0,
                                    pattern=[[0, H], [-1, NQ]], channel_multiplier=1))
            for r, s in enumerate(SHIFTS):
                pool.memset(powc[:, r:r + 1], float(2 ** s))
            pool.memset(valid[:, 0:7], 1.0)
            pool.iota(pj[:, :], pattern=[[0, 16]], base=0, channel_multiplier=1).then_inc(sem("consts"), 1)

            pool.wait_ge(sem("folds0"), 8)

            def split_expert(e):
                least(pool, sem("w_lo"), 2 * e)
                apart(pool, sem("ident"))
                for k, (w, ws) in enumerate(((W1[e], W1s), (W2[e].rearrange("(k p) c -> p k c", p=P), W2s))):
                    dst = stage[:, k, :]
                    if k:
                        dst = dst.rearrange("p (k c) -> p k c", c=C)
                    pool.dma_start(dst, w).then_inc(sem(f"ld_stage{k}"), 16)
                for k, ws in enumerate((W1s, W2s)):
                    pool.wait_ge(sem(f"ld_stage{k}"), 16 * (e + 1))
                    pool.tensor_copy(ws[:, 0, bass.ds(e * FF0, FF0)], stage[:, k, :]).then_inc(sem("w_hi"), 1)
                    pool.wait_ge(sem("w_hi"), 2 * e + (k + 1))
                    pool.tensor_tensor(ws[:, 1, bass.ds(e * FF0, FF0)], stage[:, k, :],
                                       ws[:, 0, bass.ds(e * FF0, FF0)], ALU.subtract).then_inc(sem("w_lo"), 1)
            first_loop_last(pool, E, split_expert)

            for L, units in ((0, 8), (1, 4)):
                def lows(e):
                    for k in range(units):
                        pool.wait_ge(sem(f"f{L}_hi"), units * e + (k + 1))
                        pool.tensor_tensor(hid_s[:, 1, k % 4, :], hid[:, k % 4, :], hid_s[:, 0, k % 4, :],
                                           ALU.subtract).then_inc(sem(f"f{L}_lo"), 1)
                first_loop_last(pool, E, lows)

        def head_view(a, h, half):
            v = qo[:, a, :].rearrange("c (b h q) -> c b h q", h=H, q=NQ)
            return v[:, 8 * half:8 * half + 8, h, :]

        def three(pe, dst, w, m, start=True, stop=True):
            pe.matmul(dst, w(0), m(0), start=start, stop=False, skip_group_check=True)
            pe.matmul(dst, w(0), m(1), start=False, stop=False, skip_group_check=True)
            return pe.matmul(dst, w(1), m(0), start=False, stop=stop, skip_group_check=True)

        def pe_norm(pe, k):
            for h in range(2):
                if k:
                    pe.wait_ge(sem(f"x_{k}"), h + 1)
                pe.matmul(bank(h, HALF), mean_w[:, :], xT[:, HALF * h:HALF * (h + 1)],
                          start=True, stop=True).then_inc(sem(f"n{k}_mean"), 1)
            for h in range(2):
                pe.wait_ge(sem(f"n{k}_sq"), h + 1)
                pe.matmul(bank(2 + h, HALF), mean_w[:, :], sq[:, HALF * h:HALF * (h + 1)],
                          start=True, stop=True).then_inc(sem(f"n{k}_var"), 1)

        def pe_fold_queries(pe, L):
            pe.wait_ge(sem(f"n{L * 2}_lo"), 2)
            if L == 0:
                pe.wait_ge(sem("M0"), 4)
            else:
                pe.wait_ge(sem("folds1"), 8)

            def two_heads(i):
                for k in range(4):
                    h, half = 2 * i + k // 2, k % 2
                    least(pe, sem(f"q{L}_lo"), 4 * i + (k - 3))
                    three(pe, bank(4 + k, HALF), lambda a: Ms[:, a, bass.ds(h * C, C)],
                          lambda a: xn_s[:, a, HALF * half:HALF * (half + 1)]).then_inc(sem(f"q{L}"), 1)
            first_loop_last(pe, H // 2, two_heads)

        def scores_bank(pe, L, s, n, j):
            parity = (n // TILES) % 2
            mask = L == 1
            for k, (a, b) in enumerate(((0, 0), (0, 1), (1, 0))):
                last = pe.matmul(bank(j, BANKK), qo[:, a, bass.ds(s * P, P)], cT[:, parity, b, BANKK * j:BANKK * (j + 1)],
                                 start=k == 0, stop=k == 2 and not mask)
            if mask:
                t = n % TILES
                last = pe.matmul(bank(j, BANKK), rep[:, t * P:(t + 1) * P], mbias[:, BANKK * j:BANKK * (j + 1)],
                                 start=False, stop=True)
            last.then_inc(sem(f"a{L}_S"), 1)

        def pe_step(pe, L, i, n):
            s = PAIR * i + n
            t, parity = n % TILES, (n // TILES) % 2
            final = isinstance(s, int) and s == STEPS - 1
            initial = isinstance(s, int) and s == 0
            for j in range(3):
                pe.wait_ge(sem(f"a{L}_E"), 3 * s + (j + 1))
                if not final:
                    if j == 0 and n % TILES == TILES - 1:
                        pe.wait_ge(sem(f"cT{L}"), 4 * (2 * i + (n // TILES + 1)))
                    scores_bank(pe, L, s + 1, (n + 1) % PAIR, j)
                if j == 0 and not initial:
                    pe.wait_ge(sem(f"a{L}_pTd"), 2 * s)
                    pe.wait_ge(sem(f"a{L}_pTa"), s)
                for c in range(4):
                    k = 4 * j + c
                    last = pe.transpose(bank(3 + j)[0:KP, c * P:(c + 1) * P], pr[:, n % 2, k * KP:(k + 1) * KP], ident[:, :])
                last.then_inc(sem(f"a{L}_T"), 1)
            if not initial:
                pe.wait_ge(sem(f"a{L}_on"), s)
                if 2 <= t <= 5 and not (L == 1 and isinstance(i, int) and i == NB // 2 - 1 and n >= TILES):
                    if t == 2:
                        b1_ = 2 * i + (n // TILES + 1)
                        pe.wait_ge(sem("ld_cx"), 16 * (16 * L + 1) + 16 * b1_)
                    for c in range(3):
                        k = 3 * (t - 2) + c
                        pe.transpose(bank(6 + (n + 1) % 2)[:, c * KP:(c + 1) * KP],
                                     cx[:, 1 - parity, k * C:(k + 1) * C], ident[0:KP, 0:KP])
                pe.transpose(bank(6 + (n + 1) % 2)[:, 384:512], o_n[:, (n + 1) % 2, :], ident[:, :]
                             ).then_inc(sem(f"a{L}_OT"), 1)
            if isinstance(s, int):
                least(pe, sem(f"a{L}_olo"), s - 1)
            else:
                pe.wait_ge(sem(f"a{L}_olo"), s - 1)
            for k in range(KC):
                if k == 0:
                    pe.wait_ge(sem(f"a{L}_pTd"), 2 * s + 1)
                if k == 4:
                    pe.wait_ge(sem(f"a{L}_pTa"), s + 1)
                if k == 8:
                    pe.wait_ge(sem(f"a{L}_pTd"), 2 * s + 2)
                last = pe.matmul(bank(6 + n % 2)[:, 384:512], pT[:, k * P:(k + 1) * P], cx[:, parity, k * C:(k + 1) * C],
                                 start=k == 0, stop=k == KC - 1)
            last.then_inc(sem(f"a{L}_O"), 1)

        def pe_attention(pe, L):
            pe.wait_ge(sem(f"q{L}_lo"), 2 * H)
            if L == 1:
                pe.wait_ge(sem("mbias"), 1)
            for j in range(3):
                scores_bank(pe, L, 0, 0, j)

            def pair(i):
                for n in range(PAIR):
                    pe_step(pe, L, i, n)
            first_loop_last(pe, NB // 2, pair)
            pe.wait_ge(sem(f"a{L}_on"), STEPS)
            pe.transpose(bank(6 + (STEPS - 1) % 2)[:, 384:512], o_n[:, (STEPS - 1) % 2, :], ident[:, :]
                         ).then_inc(sem(f"a{L}_OT"), 1)

        def pe_project(pe, L):
            pe.wait_ge(sem(f"a{L}_olo"), STEPS)
            if L == 0:
                pe.wait_ge(sem("N0"), 4)
            for half in range(2):
                for h in range(H):
                    last = three(pe, bank(4 + half, HALF).rearrange("p (b q) -> p b q", q=NQ), lambda a: Ns[:, a, h * C:(h + 1) * C],
                                 lambda a: head_view(a, h, half), start=h == 0, stop=h == H - 1)
                last.then_inc(sem(f"proj{L}"), 1)

        def pe_experts(pe, L):
            units = 8 if L == 0 else 4
            pe.wait_ge(sem(f"n{2 * L + 1}_lo"), 2)

            def up(e, v):
                k = v % units
                de = v // units
                f, half = k // 2, k % 2
                m = lambda a: xn_s[:, a, HALF * half:HALF * (half + 1)]
                if L == 0:
                    least(pe, sem("f0_h"), 8 * e + (v - 3))
                    last = three(pe, bank(2 + k % 4, HALF), lambda a: W1s[:, a, bass.ds(e * FF0 + (de * FF0 + f * P), P)], m)
                else:
                    least(pe, sem("f1_h"), 4 * e + (v - 1))
                    three(pe, bank(4 + k % 2, HALF), lambda a: V1s[:, a, bass.ds(e * 512 + (de * 512 + FF1 + f * P), P)], m)
                    last = three(pe, bank(2 + k % 2, HALF), lambda a: V1s[:, a, bass.ds(e * 512 + (de * 512 + f * P), P)], m)
                last.then_inc(sem(f"f{L}_up"), 1)

            def expert(e):
                for k in range(units):
                    if not (isinstance(e, int) and e == E - 1 and k >= units - 2):
                        up(e, k + 2)
                    pe.wait_ge(sem(f"f{L}_lo"), units * e + (k + 1))
                    f, half = k // 2, k % 2
                    if f == 0:
                        least(pe, sem(f"f{L}_y"), 2 * e + (half - 1))
                    ws, width = (W2s, FF0) if L == 0 else (V2s, FF1)
                    three(pe, bank(6 + half, HALF), lambda a: ws[:, a, bass.ds(e * width + f * P, P)],
                          lambda a: hid_s[:, a, k % 4, :], start=f == 0, stop=f == units // 2 - 1
                          ).then_inc(sem(f"f{L}_Y"), 1)
                    if L == 0 and k == 4:
                        pe.wait_ge(sem("tk_flag"), e + 1)
                        pe.matmul(bank(0, 1), block1[:, :], flag[:, 0:1], start=True, stop=True).then_inc(sem("tk_sum"), 1)
            if L == 0:
                pe.wait_ge(sem("w_lo"), 2 * E)
            up(0, 0)
            up(0, 1)
            first_loop_last(pe, E, expert)
            pe.wait_ge(sem(f"g{L}"), 1)
            for e in range(E):
                for half in range(2):
                    k = 2 * e + half
                    least(pe, sem(f"c{L}"), k - 1)
                    w = (ident[:, 16 * e:16 * e + 1] if L == 0 else ident[0:E, e:e + 1]).broadcast_to([P if L == 0 else E, P])
                    m = sel[:, HALF * half:HALF * (half + 1)] if L == 0 else sel[0:E, HALF * half:HALF * (half + 1)]
                    pe.matmul(bank(half, HALF), w, m, start=True, stop=True).then_inc(sem(f"gb{L}"), 1)

        @block.tensor
        def _(pe):
            pe.wait_ge(sem("ident"), 1)
            for k, (load, srcs, rows, f32, split, col) in enumerate(groups):
                pe.wait_ge(sem(load), 16)
                if k >= 8:
                    pe.wait_ge(sem("prep_a"), k - 7)
                    if groups[k - 8][4] is not None:
                        pe.wait_ge(sem("prep_d"), split_before[k - 7])
                for c, src in enumerate(srcs):
                    last = pe.transpose(bank(k % 8)[:, c * rows:(c + 1) * rows], src, ident[0:rows, 0:rows])
                last.then_inc(sem("prep"), 1)
            pe.wait_ge(sem("prep_a"), NG)
            pe.wait_ge(sem("prep_d"), split_before[NG])
            pe.wait_ge(sem("ld_Wo"), 16)
            for g in range(8):
                wl, wr = (WqT, WkT) if g < 4 else (WvT, raw["Wo"].rearrange("p (j c) -> p j c", c=C))
                for c in range(4):
                    h = 8 * (g % 4 // 2) + 2 * c + g % 2
                    r = slice(64 * (h % 2), 64 * (h % 2) + 64)
                    last = pe.matmul(bank(g)[:, c * C:(c + 1) * C], wl[r, h // 2, :], wr[r, h // 2, :], start=True, stop=True)
                last.then_inc(sem("fold_mm"), 1)
            pe.wait_ge(sem("M0"), 4)
            pe.wait_ge(sem("ld_small"), 160)
            pe.wait_ge(sem("prod"), 2)
            for h in range(H):
                r = slice(64 * (h % 2), 64 * (h % 2) + 64)
                pe.matmul(bank(h % 2)[:, h:h + 1], WkT[r, h // 2, :], bias_c[r, BQ + h // 2:BQ + h // 2 + 1], start=True, stop=True)
                pe.matmul(bank(h % 2)[:, 16 + h:17 + h], WqT[r, h // 2, :], bias_c[r, BK + h // 2:BK + h // 2 + 1], start=True, stop=True)
            for j in range(8):
                pe.matmul(bank(0)[:, 32:33], raw["Wo"][:, C * j:C * (j + 1)], bias_c[:, BV + j:BV + j + 1],
                          start=j == 0, stop=j == 7)
            pe.wait_ge(sem("consts"), 1)
            pe.matmul(bank(0)[0:H, 33:34], prod[:, :], ones_c[:, :], start=True, stop=True).then_inc(sem("bias_mm"), 1)
            pe.wait_ge(sem("bias_cols"), 1)
            pe_norm(pe, 0)
            pe.wait_ge(sem("n0_lo"), 2)
            for half in range(2):
                pe.matmul(bank(half, HALF, H), U[:, :], xn[:, HALF * half:HALF * (half + 1)],
                          start=True, stop=True).then_inc(sem("r_mm"), 1)
            pe_fold_queries(pe, 0)
            pe.wait_ge(sem("r_in"), 16)
            pe.wait_ge(sem("r_rows"), 2)
            pe.transpose(bank(0)[:, 0:STEPS], rtile[:, :], ident[0:STEPS, 0:STEPS]).then_inc(sem("r_T"), 1)
            pe.wait_ge(sem("rcol"), 1)
            pe_attention(pe, 0)
            pe_project(pe, 0)
            pe_norm(pe, 1)
            pe.wait_ge(sem("n1_lo"), 2)
            for half in range(2):
                pe.matmul(bank(half, HALF), Wg_rep[:, :, :].rearrange("p e j -> p (e j)"),
                          xn[:, HALF * half:HALF * (half + 1)], start=True, stop=True).then_inc(sem("z"), 1)
            pe_experts(pe, 0)
            pe.wait_ge(sem("x_2"), 2)
            pe.wait_ge(sem("ld_l1"), 64)
            pe.transpose(bank(0)[:, 0:C], wl1[:, 3, :], ident[:, :]).then_inc(sem("woT_mm"), 1)
            for g in range(8):
                pe.wait_ge(sem("heads_m"), 1 + g // 4)
                if g >= 4:
                    pe.wait_ge(sem("folds1"), g - 3)
                w, m = (wl1[:, 0, :], wk_m) if g < 4 else (wl1[:, 2, :], wo_m)
                pe.matmul(bank(4 + g % 4), w, m[:, 512 * (g % 4):512 * (g % 4 + 1)], start=True, stop=True
                          ).then_inc(sem("fold1_mm"), 1)
            pe_norm(pe, 2)
            pe_fold_queries(pe, 1)
            pe_attention(pe, 1)
            pe_project(pe, 1)
            pe_norm(pe, 3)
            pe.wait_ge(sem("n3_lo"), 2)
            for t in range(7):
                last = pe.matmul(bank(0)[:, E * t:E * (t + 1)], xn[:, P * t:P * (t + 1)], Wr_T[:, :], start=True, stop=True)
            last.then_inc(sem("lg"), 1)
            pe.wait_ge(sem("rw"), 1)
            for t in range(7):
                last = pe.transpose(bank(t // 4)[0:E, P * (t % 4):P * (t % 4 + 1)], tmp[:, E * t:E * (t + 1)], ident[:, :])
            last.then_inc(sem("rw_T"), 1)
            pe.wait_ge(sem("g1"), 1)
            pe_experts(pe, 1)
            pe.wait_ge(sem("x_4"), 2)
            for t in range(7):
                last = pe.transpose(bank(t // 4)[:, P * (t % 4):P * (t % 4 + 1)], xT[:, P * t:P * (t + 1)], ident[:, :])
                if t in (3, 6):
                    last.then_inc(sem("xT_rows"), 1)

        def act_norm(act, k):
            for h in range(2):
                act.wait_ge(sem(f"n{k}_var"), h + 1)
                act.activation(sq[:, HALF * h:HALF * (h + 1)], bank(2 + h, HALF), ACT.Sqrt, bias=eps_c[:, :]
                               ).then_inc(sem(f"n{k}_sd"), 1)
            for h in range(2):
                act.wait_ge(sem(f"n{k}_xn"), h + 1)
                act.activation(xn_s[:, 0, HALF * h:HALF * (h + 1)], xn[:, HALF * h:HALF * (h + 1)], ACT.Copy
                               ).then_inc(sem(f"n{k}_hi"), 1)

        def act_fold_queries(act, L):
            def two_heads(i):
                for k in range(4):
                    h, half = 2 * i + k // 2, k % 2
                    act.wait_ge(sem(f"q{L}"), 4 * i + (k + 1))
                    apart(act, sem("prep"))
                    act.activation(head_view(0, h, half) if isinstance(h, int) else dyn_head(0, h, half),
                                   bank(4 + k, HALF).rearrange("p (b q) -> p b q", q=NQ),
                                   ACT.Identity, bias=qbias[:, L, bass.ds(h, 1)]).then_inc(sem(f"q{L}_hi"), 1)
            first_loop_last(act, H // 2, two_heads)

        def dyn_head(a, h, half):
            v = qo[:, a, :].rearrange("c (b n) -> c b n", n=H * NQ)
            return v[:, 8 * half:8 * half + 8, bass.ds(h * NQ, NQ)]

        def act_exp(act, L, s, n):
            act.wait_ge(sem(f"a{L}_nb"), s + 1)
            for j in range(3):
                act.activation(pr[:, n % 2, BANKK * j:BANKK * (j + 1)], bank(j, BANKK), ACT.Exp, bias=nb[:, n % 2:n % 2 + 1],
                               accum_out=sums[:, n % 2, j:j + 1]).then_inc(sem(f"a{L}_E"), 1)

        def context_share(L, i, n):
            t = n % TILES
            if not 2 <= t <= 5 or (L == 1 and isinstance(i, int) and i == NB // 2 - 1 and n >= TILES):
                return None
            return 1 - (n // TILES) % 2, 3 * KP * (t - 2)

        def act_out_hi(act, L, i, n):
            s = PAIR * i + n
            act.wait_ge(sem(f"a{L}_OT"), s)
            b = bank(6 + (n + 1) % 2)
            share = context_share(L, i, n)
            if share:
                act.activation(cT[:, share[0], 0, share[1]:share[1] + 3 * KP], b[:, 0:3 * KP], ACT.Copy)
            else:
                apart(act, sem("prep"))
            act.activation(qo[:, 0, bass.ds(s * P - P, P)], b[:, 384:512], ACT.Copy).then_inc(sem(f"a{L}_ohi"), 1)

        def act_attention(act, L):
            act_exp(act, L, 0, 0)

            def pair(i):
                for n in range(PAIR):
                    s = PAIR * i + n
                    act.wait_ge(sem(f"a{L}_T"), 3 * s + 2)
                    act.activation(pT[:, 4 * P:8 * P], bank(4)[0:KP, :], ACT.Copy).then_inc(sem(f"a{L}_pTa"), 1)
                    if not (isinstance(s, int) and s == 0):
                        act_out_hi(act, L, i, n)
                    if not (isinstance(s, int) and s == STEPS - 1):
                        act_exp(act, L, s + 1, (n + 1) % PAIR)
                    act.wait_ge(sem(f"a{L}_O"), s + 1)
                    act.wait_ge(sem(f"a{L}_rd"), s + 1)
                    act.activation(o_n[:, n % 2, :], bank(6 + n % 2)[:, 384:512], ACT.Copy, scale=den[:, n % 2:n % 2 + 1]
                                   ).then_inc(sem(f"a{L}_on"), 1)
            first_loop_last(act, NB // 2, pair)
            act.wait_ge(sem(f"a{L}_OT"), STEPS)
            act.activation(qo[:, 0, (STEPS - 1) * P:STEPS * P], bank(6 + (STEPS - 1) % 2)[:, 384:512], ACT.Copy
                           ).then_inc(sem(f"a{L}_ohi"), 1)

        def act_experts(act, L):
            units = 8 if L == 0 else 4

            def hidden(e, v):
                k, de = v % units, v // units
                f, half = k // 2, k % 2
                act.wait_ge(sem(f"f{L}_up"), units * e + (v + 1))
                if L == 0:
                    act.activation(hid[:, k % 4, :], bank(2 + k % 4, HALF), ACT.Gelu,
                                   bias=b1_now[:, 4 * de + f:4 * de + f + 1]).then_inc(sem("f0_h"), 1)
                else:
                    least(act, sem("f1_h"), 4 * e + (v - 1))
                    act.activation(sel_silu(k % 2), bank(4 + k % 2, HALF), ACT.Silu).then_inc(sem("f1_silu"), 1)

            def biases(e):
                act.wait_ge(sem("b1_now"), e + 1)

            def expert(e):
                if L == 0 and not (isinstance(e, int) and e == 0):
                    biases(e)
                for k in range(units):
                    if not (isinstance(e, int) and e == E - 1 and k >= units - 2):
                        hidden(e, k + 2)
                    if k >= units - 2:
                        half = k % 2
                        act.wait_ge(sem(f"f{L}_Y"), units * e + (k + 1))
                        apart(act, sem("prep"))
                        if L == 0:
                            act.activation(y_e[:, bass.ds(e * TOK + HALF * half, HALF)], bank(6 + half, HALF), ACT.Identity,
                                           bias=b2c[:, bass.ds(e, 1)]).then_inc(sem("f0_y"), 1)
                        else:
                            act.activation(y_e[:, bass.ds(e * TOK + HALF * half, HALF)], bank(6 + half, HALF), ACT.Copy
                                           ).then_inc(sem("f1_y"), 1)
            if L == 0:
                biases(0)
            hidden(0, 0)
            hidden(0, 1)
            first_loop_last(act, E, expert)

        def sel_silu(k):
            return sq[:, HALF * k:HALF * (k + 1)]

        def half_of(t, h):
            return t[:, HALF * h:HALF * (h + 1)]

        @block.scalar
        def _(act):
            for k, (load, srcs, rows, f32, split, col) in enumerate(groups):
                act.wait_ge(sem("prep"), k + 1)
                n = rows * len(srcs)
                src = bank(k % 8, n)
                if f32 is not None:
                    if len(f32.shape) == 3:
                        src = src.rearrange("p (j c) -> p j c", c=C)
                    act.activation(f32, src, ACT.Copy).then_inc(sem("prep_a"), 1)
                else:
                    act.activation(split[:, 0, col:col + n], src, ACT.Copy).then_inc(sem("prep_a"), 1)
            for g in range(8):
                act.wait_ge(sem("fold_mm"), g + 1)
                dst, scale = (Ms, DH0 ** -0.5) if g < 4 else (Ns, 1.0)
                act.activation(fold_part(dst, 0, g), bank(g).rearrange("p (c n) -> p c n", n=C), ACT.Copy, scale=scale
                               ).then_inc(sem("fold_hi"), 1)
            act.wait_ge(sem("ld_small"), 160)
            act.wait_ge(sem("b1_pad"), 1)
            act.activation(gates[:, :], gates[:, :], ACT.Tanh).then_inc(sem("tanh"), 1)
            act_norm(act, 0)
            for half in range(2):
                act.wait_ge(sem("r_mm"), half + 1)
                act.wait_ge(sem("bias_cols"), 1)
                act.activation(rrow[:, HALF * half:HALF * (half + 1)], bank(half, HALF, H), ACT.Identity, bias=crow[:, :]
                               ).then_inc(sem("r_rows"), 1)
            act_fold_queries(act, 0)
            act_attention(act, 0)
            act_norm(act, 1)
            for half in range(2):
                act.wait_ge(sem("z"), half + 1)
                act.activation(half_of(sig, half), bank(half, HALF), ACT.Exp, scale=-1.0).then_inc(sem("ez"), 1)
            act_experts(act, 0)
            for g in range(8):
                act.wait_ge(sem("fold1_mm"), g + 1)
                dst, scale = (Ms, DH1 ** -0.5) if g < 4 else (Ns, 1.0)
                act.activation(dst[:, 0, 512 * (g % 4):512 * (g % 4 + 1)], bank(4 + g % 4), ACT.Copy, scale=scale
                               ).then_inc(sem("fold1_hi"), 1)
            act_norm(act, 2)
            act_fold_queries(act, 1)
            act_attention(act, 1)
            act_norm(act, 3)
            act.wait_ge(sem("lg_rel"), 1)
            act.activation(half_of(acc, 0)[:, 0:56], half_of(tmp, 0)[:, 64:120], ACT.Exp).then_inc(sem("lg_exp"), 1)
            act_experts(act, 1)

        @block.vector
        def _(dve):
            chain = [0]

            def link(ins):
                chain[0] += 1
                ins.then_inc(sem("dve_chain"), 1)
                dve.wait_ge(sem("dve_chain"), chain[0])

            def minus(dst, src, hi, scale=None):
                if scale is None:
                    return dve.tensor_tensor(dst, src, hi, ALU.subtract)
                return dve.scalar_tensor_tensor(dst, src, scale, hi, ALU.mult, ALU.subtract)

            def norm(k):
                for h in range(2):
                    dve.wait_ge(sem(f"n{k}_mean"), h + 1)
                    link(dve.tensor_tensor(half_of(xn, h), half_of(xT, h), bank(h, HALF), ALU.subtract))
                    dve.tensor_tensor(half_of(sq, h), half_of(xn, h), half_of(xn, h), ALU.mult).then_inc(sem(f"n{k}_sq"), 1)
                for h in range(2):
                    dve.wait_ge(sem(f"n{k}_sd"), h + 1)
                    link(dve.reciprocal(half_of(sq, h), half_of(sq, h)))
                    dve.tensor_tensor(half_of(xn, h), half_of(xn, h), half_of(sq, h), ALU.mult).then_inc(sem(f"n{k}_xn"), 1)
                for h in range(2):
                    dve.wait_ge(sem(f"n{k}_hi"), h + 1)
                    minus(half_of(xn_s[:, 1, :], h), half_of(xn, h), half_of(xn_s[:, 0, :], h)).then_inc(sem(f"n{k}_lo"), 1)

            def fold_queries(L):
                def two_heads(i):
                    for k in range(4):
                        h, half = 2 * i + k // 2, k % 2
                        dve.wait_ge(sem(f"q{L}_hi"), 4 * i + (k + 1))
                        dve.scalar_tensor_tensor(dyn_head(1, h, half), bank(4 + k, HALF).rearrange("p (b q) -> p b q", q=NQ),
                                                 qbias[:, L, bass.ds(h, 1)], dyn_head(0, h, half), ALU.add, ALU.subtract
                                                 ).then_inc(sem(f"q{L}_lo"), 1)
                first_loop_last(dve, H // 2, two_heads)

            def maxima(L, s, n, part):
                if part == 0:
                    dve.wait_ge(sem(f"a{L}_S"), 3 * s + 2)
                    src = ps[:, 0:1024].rearrange("p (j k) -> p j k", k=512)[:, :, 0:BANKK]
                    dve.tensor_reduce(mx[:, 0:1], src, mybir.AxisListType.XY, ALU.max).then_inc(sem(f"a{L}_m"), 1)
                    return
                dve.wait_ge(sem(f"a{L}_S"), 3 * s + 3)
                dve.reduce_max(mx[:, 1:2], bank(2, BANKK), AX).then_inc(sem(f"a{L}_m"), 1)
                if L == 0:
                    dve.wait_ge(sem("a0_m"), 3 * s + 2)
                    dve.tensor_scalar(mx[:, 2:3], mx[:, 0:1], mx[:, 1:2], rcol[:, bass.ds(s, 1)], ALU.max, ALU.add
                                      ).then_inc(sem("a0_m"), 1)
                    dve.wait_ge(sem("a0_m"), 3 * s + 3)
                    dve.tensor_scalar(nb[:, n % 2:n % 2 + 1], mx[:, 2:3], rcol[:, bass.ds(s, 1)], -1.0, ALU.subtract, ALU.mult
                                      ).then_inc(sem("a0_nb"), 1)
                else:
                    dve.wait_ge(sem("a1_m"), 2 * s + 2)
                    dve.tensor_scalar(nb[:, n % 2:n % 2 + 1], mx[:, 0:1], mx[:, 1:2], -1.0, ALU.max, ALU.mult
                                      ).then_inc(sem("a1_nb"), 1)

            def out_lo(L, i, n):
                s = PAIR * i + n
                dve.wait_ge(sem(f"a{L}_ohi"), s)
                b = bank(6 + (n + 1) % 2)
                share = context_share(L, i, n)
                if share:
                    cols_ = slice(share[1], share[1] + 3 * KP)
                    minus(cT[:, share[0], 1, cols_], b[:, 0:3 * KP], cT[:, share[0], 0, cols_]).then_inc(sem(f"cT{L}"), 1)
                minus(qo[:, 1, bass.ds(s * P - P, P)], b[:, 384:512], qo[:, 0, bass.ds(s * P - P, P)]).then_inc(sem(f"a{L}_olo"), 1)

            def attention(L):
                maxima(L, 0, 0, 0)
                maxima(L, 0, 0, 1)

                def pair(i):
                    for n in range(PAIR):
                        s = PAIR * i + n
                        final = isinstance(s, int) and s == STEPS - 1
                        dve.wait_ge(sem(f"a{L}_T"), 3 * s + 1)
                        dve.tensor_copy(pT[:, 0:4 * P], bank(3)[0:KP, :]).then_inc(sem(f"a{L}_pTd"), 1)
                        if not final:
                            maxima(L, s + 1, (n + 1) % PAIR, 0)
                            maxima(L, s + 1, (n + 1) % PAIR, 1)
                        dve.wait_ge(sem(f"a{L}_T"), 3 * s + 3)
                        dve.tensor_copy(pT[:, 8 * P:12 * P], bank(5)[0:KP, :]).then_inc(sem(f"a{L}_pTd"), 1)
                        dve.tensor_reduce(cols[:, n % 2:n % 2 + 1], sums[:, n % 2, :], AX, ALU.add).then_inc(sem(f"a{L}_den"), 1)
                        dve.wait_ge(sem(f"a{L}_den"), s + 1)
                        dve.reciprocal(den[:, n % 2:n % 2 + 1], cols[:, n % 2:n % 2 + 1]).then_inc(sem(f"a{L}_rd"), 1)
                        if not (isinstance(s, int) and s == 0):
                            out_lo(L, i, n)
                first_loop_last(dve, NB // 2, pair)
                dve.wait_ge(sem(f"a{L}_ohi"), STEPS)
                last = slice((STEPS - 1) * P, STEPS * P)
                minus(qo[:, 1, last], bank(6 + (STEPS - 1) % 2)[:, 384:512], qo[:, 0, last]).then_inc(sem(f"a{L}_olo"), 1)

            def residual(L, k):
                for h in range(2):
                    dve.wait_ge(sem(f"proj{L}"), h + 1)
                    if L == 0:
                        link(dve.tensor_scalar(half_of(sq, h), bank(4 + h, HALF), bias_c[:, OB:OB + 1], gates[:, 0:1],
                                               ALU.add, ALU.mult))
                    else:
                        link(dve.tensor_scalar(half_of(sq, h), bank(4 + h, HALF), gates[:, 1:2], None, ALU.mult))
                    dve.tensor_tensor(half_of(xT, h), half_of(xT, h), half_of(sq, h), ALU.add).then_inc(sem(f"x_{k}"), 1)

            def experts(L, round_of=None):
                units = 8 if L == 0 else 4

                def high(e, v):
                    k, de = v % units, v // units
                    if L == 1:
                        dve.wait_ge(sem("f1_silu"), 4 * e + (v + 1))
                        least(dve, sem("f1_lo"), 4 * e + (v - 3))
                        dve.tensor_tensor(hid[:, k % 4, :], bank(2 + k % 2, HALF), sel_silu(k % 2), ALU.mult
                                          ).then_inc(sem("f1_h"), 1)
                    dve.wait_ge(sem(f"f{L}_h"), units * e + (v + 1))
                    least(dve, sem(f"f{L}_Y"), units * e + (v - 3))
                    dve.tensor_copy(hid_s[:, 0, k % 4, :], hid[:, k % 4, :]).then_inc(sem(f"f{L}_hi"), 1)

                def biases(e):
                    dve.wait_ge(sem("f0_h"), 8 * e + 2)
                    dve.tensor_scalar(b1_now[:, :], b1c[:, bass.ds(4 * e, 8)], 0.0, None, ALU.add).then_inc(sem("b1_now"), 1)

                def expert(e):
                    if L == 0 and not (isinstance(e, int) and e == 0):
                        biases(e)
                    for k in range(units):
                        if not (isinstance(e, int) and e == E - 1 and k >= units - 2):
                            high(e, k + 2)
                        if round_of:
                            round_of(e, k)
                if L == 0:
                    dve.tensor_scalar(b1_now[:, :], b1c[:, 0:8], 0.0, None, ALU.add).then_inc(sem("b1_now"), 1)
                high(0, 0)
                high(0, 1)
                first_loop_last(dve, E, expert)

            def tk_round(e, k):
                if k == 0:
                    dve.tensor_tensor(cand[:, :], prefix[:, :], jsh[:, bass.ds(e, 1)], ALU.bitwise_or).then_inc(sem("tk"), 1)
                if k == 1:
                    dve.wait_ge(sem("tk"), 5 * e + 1)
                    dve.tensor_scalar(tmp, sig, cand[:, :].bitcast(F32), 0.0, ALU.is_ge, ALU.add, accum_out=flag[:, 1:2]
                                      ).then_inc(sem("tk"), 1)
                if k == 2:
                    dve.wait_ge(sem("tk"), 5 * e + 2)
                    dve.tensor_scalar(flag[:, 0:1], flag[:, 1:2], float(TOPK), valid[:, bass.ds(e, 1)], ALU.is_ge, ALU.mult
                                      ).then_inc(sem("tk_flag"), 1)
                if k == 5:
                    dve.wait_ge(sem("tk_sum"), e + 1)
                    dve.tensor_scalar(digit[:, 0:1], bank(0, 1), -1.0, powc[:, bass.ds(e, 1)], ALU.add, ALU.mult
                                      ).then_inc(sem("tk"), 1)
                if k == 6:
                    dve.wait_ge(sem("tk"), 5 * e + 3)
                    dve.tensor_copy(digit_i[:, :], digit[:, 0:1]).then_inc(sem("tk"), 1)
                if k == 7:
                    dve.wait_ge(sem("tk"), 5 * e + 4)
                    dve.tensor_tensor(prefix[:, :], prefix[:, :], digit_i[:, :], ALU.bitwise_or).then_inc(sem("tk"), 1)
                    dve.wait_ge(sem("tk"), 5 * e + 5)

            def combine(L, k):
                for e in range(E):
                    for h in range(2):
                        dve.wait_ge(sem(f"gb{L}"), 2 * e + h + 1)
                        dve.wait_ge(sem(f"f{L}_y"), 2 * E)
                        y = y_e[:, e * TOK + HALF * h:e * TOK + HALF * (h + 1)]
                        if e == 0:
                            dve.tensor_tensor(half_of(acc, h), y, bank(h, HALF), ALU.mult).then_inc(sem(f"c{L}"), 1)
                            dve.wait_ge(sem(f"c{L}"), 2 * e + h + 1)
                        else:
                            dve.tensor_tensor(y, y, bank(h, HALF), ALU.mult).then_inc(sem(f"c{L}"), 1)
                            dve.wait_ge(sem(f"c{L}"), 2 * e + h + 1)
                            link(dve.tensor_tensor(half_of(acc, h), half_of(acc, h), y, ALU.add))
                for h in range(2):
                    dve.scalar_tensor_tensor(half_of(xT, h), half_of(acc, h), gates[:, 2 + L:3 + L], half_of(xT, h),
                                             ALU.mult, ALU.add).then_inc(sem(f"x_{k}"), 1)

            for k, (load, srcs, rows, f32, split, col) in enumerate(groups):
                if split is None:
                    continue
                dve.wait_ge(sem("prep_a"), k + 1)
                n = rows * len(srcs)
                minus(split[:, 1, col:col + n], bank(k % 8, n), split[:, 0, col:col + n]).then_inc(sem("prep_d"), 1)
            for g in range(8):
                dve.wait_ge(sem("fold_hi"), g + 1)
                dst, scale = (Ms, DH0 ** -0.5) if g < 4 else (Ns, 1.0)
                last = minus(fold_part(dst, 1, g), bank(g).rearrange("p (c n) -> p c n", n=C), fold_part(dst, 0, g), scale)
                last.then_inc(sem("M0" if g < 4 else "N0"), 1)
                if g == 3:
                    dve.wait_ge(sem("ld_small"), 160)
                    dve.wait_ge(sem("consts"), 1)
                    for s_ in range(2):
                        r = slice(64 * s_, 64 * s_ + 64)
                        dve.tensor_tensor(prod[r, s_:H:2], bias_c[r, BQ:BQ + 8], bias_c[r, BK:BK + 8], ALU.mult).then_inc(sem("prod"), 1)
            dve.wait_ge(sem("bias_mm"), 1)
            SC = DH0 ** -0.5
            for s_ in range(2):
                dve.tensor_scalar(qbias[:, 0, s_:H:2], bank(s_)[:, s_:H:2], SC, None, ALU.mult)
                dve.tensor_scalar(U[:, s_:H:2], bank(s_)[:, 16 + s_:32:2], SC, None, ALU.mult)
            dve.tensor_scalar(crow[:, :], bank(0)[0:H, 33:34], SC, None, ALU.mult)
            link(dve.tensor_tensor(bias_c[:, OB:OB + 1], bank(0)[:, 32:33], bias_c[:, BO:BO + 1], ALU.add))
            for r, sh in enumerate(SHIFTS):
                last = dve.tensor_scalar(jsh[:, r:r + 1], pj[:, r:r + 1], 15, sh, ALU.bitwise_and, ALU.logical_shift_left)
            link(last)
            link(dve.tensor_copy(cols[:, 7:8], jsh[:, 7:8]))
            link(dve.tensor_scalar(valid[:, 7:8], cols[:, 7:8], 8.0, None, ALU.is_lt))
            link(dve.tensor_scalar(prefix[:, :], jsh[:, 0:1], 0, None, ALU.bitwise_and))
            dve.tensor_copy(Wg_rep[:, :, :], wg_raw[:, :].unsqueeze(2).broadcast_to([P, E, 16])).then_inc(sem("bias_cols"), 1)
            dve.wait_ge(sem("N0"), 4)
            dve.wait_ge(sem("M0"), 4)
            dve.sem_inc(sem("folds0"), 8)

            norm(0)
            fold_queries(0)
            dve.wait_ge(sem("r_T"), 1)
            dve.tensor_copy(rcol[:, :], bank(0)[:, 0:STEPS]).then_inc(sem("rcol"), 1)
            dve.wait_ge(sem("rcol"), 1)
            attention(0)
            dve.wait_ge(sem("tanh"), 1)
            residual(0, 1)
            norm(1)
            for h in range(2):
                dve.wait_ge(sem("ez"), h + 1)
                link(dve.tensor_scalar(half_of(sig, h), half_of(sig, h), 1.0, None, ALU.add))
                link(dve.reciprocal(half_of(sig, h), half_of(sig, h)))
            experts(0, tk_round)
            thr = prefix[:, :].bitcast(F32)
            link(dve.tensor_scalar(sel, sig, thr, 0.0, ALU.is_gt, ALU.add, accum_out=flag[:, 1:2]))
            link(dve.tensor_scalar(flag[:, 0:1], flag[:, 1:2], -1.0, float(TOPK), ALU.mult, ALU.add))
            link(dve.tensor_scalar(tmp, sig, thr, None, ALU.is_equal))
            link(dve.memset(sq[:, :], 1.0))
            link(dve.tensor_tensor_scan(acc, tmp, sq[:, :], 0.0, ALU.add, ALU.mult))
            link(dve.tensor_scalar(acc, acc, flag[:, 0:1], None, ALU.is_le))
            link(dve.tensor_tensor(tmp, tmp, acc, ALU.mult))
            link(dve.tensor_tensor(sel, sel, tmp, ALU.add))
            dve.tensor_tensor(sel, sel, sig, ALU.mult).then_inc(sem("g0"), 1)
            combine(0, 2)
            dve.wait_ge(sem("ld_l1"), 64)
            def only_heads(dst, src):
                return dve.tensor_tensor(dst.rearrange("p (h c) -> p h c", c=C), src.unsqueeze(1).broadcast_to([P, H, C]),
                                         headm[:, :].unsqueeze(2).broadcast_to([P, H, C]), ALU.mult)
            dve.wait_ge(sem("x_2"), 2)
            only_heads(wk_m, wl1[:, 1, :]).then_inc(sem("heads_m"), 1)
            dve.wait_ge(sem("woT_mm"), 1)
            link(dve.tensor_copy(woT[:, :], bank(0)[:, 0:C]))
            only_heads(wo_m, woT[:, :]).then_inc(sem("heads_m"), 1)
            dve.wait_ge(sem("ld_mask"), 16)
            dve.tensor_scalar(mbias[:, :].rearrange("q (c p) -> q c p", p=KP), mask_i.rearrange("q (p c) -> q c p", c=KC),
                              0.0, MASKED, ALU.is_equal, ALU.mult).then_inc(sem("mbias"), 1)
            for g in range(8):
                dve.wait_ge(sem("fold1_hi"), g + 1)
                dst, scale = (Ms, DH1 ** -0.5) if g < 4 else (Ns, 1.0)
                cols_ = slice(512 * (g % 4), 512 * (g % 4 + 1))
                minus(dst[:, 1, cols_], bank(4 + g % 4), dst[:, 0, cols_], scale).then_inc(sem("folds1"), 1)
            norm(2)
            fold_queries(1)
            attention(1)
            residual(1, 3)
            norm(3)
            T7 = 7
            lg = tmp[:, 0:56]
            rel = tmp[:, 64:120]
            ex = acc[:, 0:56]
            v3 = lambda a: a.rearrange("p (t e) -> p t e", e=E)
            gt = sig[:, 0:448].rearrange("p (t e j) -> p t e j", t=T7, e=E)
            eq = sig[:, 448:896].rearrange("p (t e j) -> p t e j", t=T7, e=E)
            dve.wait_ge(sem("lg"), 1)
            link(dve.tensor_copy(lg, bank(0)[:, 0:56]))
            lj = v3(lg).unsqueeze(2).broadcast_to([P, T7, E, E])
            le = v3(lg).unsqueeze(3).broadcast_to([P, T7, E, E])
            link(dve.tensor_tensor(gt, lj, le, ALU.is_gt))
            link(dve.tensor_tensor(eq, lj, le, ALU.is_equal))
            link(dve.tensor_tensor(eq, eq, tril[:, :, :].unsqueeze(1).broadcast_to([P, T7, E, E]), ALU.mult))
            link(dve.tensor_tensor(gt, gt, eq, ALU.add))
            rank = sel[:, 0:56]
            link(dve.tensor_reduce(rank, gt.rearrange("p t e j -> p (t e) j"), AX, ALU.add))
            link(dve.tensor_scalar(rank, rank, 2.0, None, ALU.is_lt))
            top = sel[:, 64:71]
            link(dve.tensor_reduce(top, v3(lg), AX, ALU.max))
            dve.tensor_tensor(v3(rel), v3(lg), top.unsqueeze(2).broadcast_to([P, T7, E]), ALU.subtract).then_inc(sem("lg_rel"), 1)
            dve.wait_ge(sem("lg_exp"), 1)
            link(dve.tensor_tensor(ex, ex, rank, ALU.mult))
            link(dve.tensor_reduce(top, v3(ex), AX, ALU.add))
            link(dve.reciprocal(top, top))
            dve.tensor_tensor(v3(lg), v3(ex), top.unsqueeze(2).broadcast_to([P, T7, E]), ALU.mult).then_inc(sem("rw"), 1)
            dve.wait_ge(sem("rw_T"), 1)
            link(dve.tensor_copy(sel[0:E, 0:512], bank(0)[0:E, :]))
            dve.tensor_copy(sel[0:E, 512:896], bank(1)[0:E, 0:384]).then_inc(sem("g1"), 1)
            experts(1)
            combine(1, 4)
            for g in range(2):
                dve.wait_ge(sem("xT_rows"), g + 1)
                n = 512 if g == 0 else 384
                dve.tensor_copy(xn[:, 512 * g:512 * g + n], bank(g, n)).then_inc(sem("out_rows"), 1)


_INS = ['x', 'ctx_1024', 'mask_1x1xSxS2_ik0', 'g_xattn', 'g_ffn', 'L0_xattn_Wq', 'L0_xattn_bq', 'L0_xattn_Wk',
        'L0_xattn_bk', 'L0_xattn_Wv', 'L0_xattn_bv', 'L0_xattn_Wo', 'L0_xattn_bo', 'L0_ffn_Wg', 'L0_ffn_W1',
        'L0_ffn_b1', 'L0_ffn_W2', 'L0_ffn_b2', 'L1_xattn_w_q', 'L1_xattn_w_k', 'L1_xattn_w_v', 'L1_xattn_w_o',
        'L1_ffn_Wr', 'L1_ffn_W1', 'L1_ffn_W2']


def kernel(**inputs):
    import numpy as _np
    import concourse.bacc as _bacc
    from concourse import mybir as _mybir
    from concourse.bass_utils import run_bass_kernel_spmd as _run

    nc = _bacc.Bacc("TRN2", target_bir_lowering=False, num_devices=1)
    arrays, args = {}, []
    for name in _INS:
        a = _np.ascontiguousarray(inputs[name])
        arrays[f"in_{name}_dram"] = a
        args.append(nc.dram_tensor(f"in_{name}_dram", a.shape, _mybir.dt.from_np(a.dtype), kind="ExternalInput").ap())
    args.append(nc.dram_tensor("out_0_dram", (NB, NQ, C), F32, kind="ExternalOutput").ap())
    flamingo(nc, *args)
    r = _run(nc, [arrays], core_ids=[0])
    return r.results[0]["out_0_dram"]
```

```python
import concourse.bass as bass
from concourse import mybir
from contextlib import ExitStack

F32 = mybir.dt.float32
BF16 = mybir.dt.bfloat16
I32 = mybir.dt.int32
ALU = mybir.AluOpType
ACT = mybir.ActivationFunctionType
AX = mybir.AxisListType.X

P = 128
NB, NQ, C = 16, 56, 128
NK = 1500
KC, KP = 12, 125
H = 16
TOK = NB * NQ
HALF = TOK // 2
TILES = H * NQ // P
STEPS = NB * TILES
PAIR = 2 * TILES
BANKK = 500
DH0, DH1 = 64, 8
E = 8
FF0, FF1 = 512, 256
TOPK = TOK * 2 // E
EPS = 1e-5
T1 = H // 2
R1 = 2 * NQ
STEPS1 = NB * T1
W1T = 2 * DH1
VW = 2 * W1T + 1
VS = VW + 1
KS_ROWS = 107
SHIFT_ROW = 96
KS_LOADS = 16 * 3
STACK = (0, 32, 64)
PARTS = ((2,), (3,), (4, 5), (6,), (7,), (8,), (0,), (1,))
MERGE = (5, 6)
MASK_ROWS = ((16, 0, 16), (48, 16, 16), (80, 32, 16), (99, 48, 8))
MASKED = -float(2 ** 100)
SHIFTS = [27, 23, 19, 15, 11, 7, 3, 0]


def least(eng, sem, value):
    if isinstance(value, int) and value <= 0:
        return
    eng.wait_ge(sem, value)


def apart(eng, done):
    eng.wait_ge(done, 1)


def first_loop_last(eng, count, body):
    body(0)
    with eng.Fori(1, count - 1) as i:
        body(i)
    body(count - 1)


def flamingo(nc, x, ctx_d, mask_d, g_xattn, g_ffn, Wq, bq, Wk, bk, Wv, bv, Wo, bo,
             Wg, W1, b1, W2, b2, w_q, w_k, w_v, w_o, Wr, V1, V2, out):
    stack = ExitStack()
    with stack:
        def sb(name, shape, dt=F32):
            return stack.enter_context(nc.sbuf_tensor(name, shape, dt))

        sems = {}

        def sem(name):
            if name not in sems:
                sems[name] = stack.enter_context(nc.semaphore(name))
            return sems[name]

        xT = sb("xT", [P, TOK])
        xn = sb("xn", [P, TOK])
        sq = sb("sq", [P, TOK])
        xn_s = sb("xn_split", [P, 2, TOK], BF16)
        qo = sb("queries_outputs", [P, 2, H * TOK], BF16)
        W12 = sb("W1_W2_split", [P, 2, 2, E * FF0], BF16)
        W1s, W2s = W12[:, 0], W12[:, 1]
        V1s = sb("V1_split", [P, 2, E * 2 * FF1], BF16)
        V2s = sb("V2_split", [P, 2, E * FF1], BF16)
        Ms = sb("M_split", [P, 2, H * C], BF16)
        Ns = sb("N_split", [P, 2, H * C], BF16)
        cx = sb("context", [KP, 2, KC * C])
        cT = sb("context_T_split", [C, 2, 2, NK], BF16)
        pr = sb("probs", [P, 2, NK])
        pT = sb("probs_T", [KP, KC * P])
        o_n = sb("outputs_scaled", [P, 2, C])
        ident = sb("ident", [P, P])
        mean_w = sb("mean_w", [P, P])
        block1 = sb("block_ones", [P, P])
        tril = sb("tril", [P, E, E])
        rep = sb("repeat_ident", [NQ, HALF], BF16)
        keep = sb("keep", [NQ, 2])
        repk = sb("repeat_keep", [NQ, HALF], BF16)
        ones_q = sb("ones_q", [NQ, P], BF16)
        place_m = sb("place_mask_rows", [NQ, 112], BF16)
        parity_c = sb("parity_columns", [P, 2])
        pick = sb("pick", [P, 2, 2, 224])
        o1 = sq[:, :].rearrange("p (a g n) -> p a g n", a=2, g=4)
        mask_ones = sb("mask_bias_and_ones", [67, NK], BF16)
        mbias = mask_ones[0:NQ]
        tail = mask_ones[64:67]
        stage = sb("stage", [P, 2, FF0])
        wl1 = sb("L1_proj", [P, 4, C])
        wl1T = sb("L1_proj_T", [P, 4, C])
        woT = wl1T[:, 3, :]
        kvs = sb("kv_split", [P, 2, 2, C], BF16)
        bias_c = sb("bias_columns", [P, 64])
        U = sb("U", [P, H])
        qbias = sb("qbias", [P, H])
        prod = sb("bq_bk", [P, H])
        rrow = sq[0:H, :]
        rtile = sb("rtile", [STEPS, P])
        rcol = sb("rcol", [P, STEPS])
        crow = sb("crow", [H, 1])
        mx = sb("mx", [P, 4])
        mh = sb("minus_max_halves", [R1, 2, 2], BF16)
        identb = sb("ident_bf16", [P, P], BF16)
        nb = sb("nb", [P, 2])
        sums = sb("sums", [P, 2, 3])
        den = sb("den", [P, 2])
        gates = sb("gates", [P, 4])
        eps_c = sb("eps", [P, 1])
        ones_c = sb("ones_c", [P, 1])
        Wg_rep = sb("Wg_rep", [P, E, 16])
        Wr_T = sb("Wr_T", [P, E])
        wg_raw = sb("Wg_raw", [P, E])
        b1c = sb("b1c", [P, E * 4 + 4])
        b1_now = sb("b1_now", [P, 8])
        b2c = sb("b2c", [P, E])
        pj = sb("pj", [P, 16], I32)
        jsh = sb("jsh", [P, 8], I32)
        powc = sb("powc", [P, 8])
        valid = sb("valid", [P, 8])
        prefix = sb("prefix", [P, 1], I32)
        cand = sb("cand", [P, 1], I32)
        digit = sb("digit", [P, 2])
        digit_i = sb("digit_i", [P, 1], I32)
        flag = sb("flag", [P, 2])
        cols = sb("cols", [P, 8])

        q32 = qo[:, :, :].rearrange("p a n -> p (a n)").bitcast(F32)
        raw = {}
        at = 0
        for name, n in (("Wq", 1024), ("Wk", 1024), ("Wv", 1024), ("Wo", 1024), ("V1", 4096), ("V2", 2048), ("x", 896)):
            raw[name] = q32[:, at:at + n]
            at += n
        pr32 = pr[:, :, :].rearrange("p a n -> p (a n)")
        WqT = pr32[:, 0:1024].rearrange("p (j c) -> p j c", c=C)
        WkT = pr32[:, 1024:2048].rearrange("p (j c) -> p j c", c=C)
        WvT = stage[:, :, :].rearrange("p a n -> p (a n)").rearrange("p (j c) -> p j c", c=C)
        y_e = q32[:, 0:E * TOK]
        scr = q32[:, E * TOK:2 * E * TOK]
        hid = scr[:, 0:1792].rearrange("p (r n) -> p r n", r=4)
        hid_s = scr[:, 1792:3584].bitcast(BF16).rearrange("p (a r n) -> p a r n", a=2, r=4)
        sig = scr[:, 3584:4480]
        tmp = scr[:, 4480:5376]
        sel = scr[:, 5376:6272]
        acc = scr[:, 6272:7168]
        qflat = qo[:, :, :].rearrange("p a n -> p (a n)")
        ks = qflat[:, 0:2 * T1 * NK].rearrange("p (a j n) -> p a j n", a=2, j=T1)
        kT = qflat[:, 2 * T1 * NK:2 * T1 * NK + 2 * NK].rearrange("p (a n) -> p a n", a=2)
        qs = W12[:, :, :, :].rearrange("p a b n -> p (a b n)")[:, 0:STEPS1 * R1]
        p_f = pT[:, 0:KC * R1]
        p_s = pr32[0:KP].bitcast(BF16)[:, 0:4 * KC * R1].rearrange("p (t a n) -> p t a n", t=2, a=2)
        vals = [m[0:KP, :, :].rearrange("p a n -> p (a n)")[:, 0:KC * T1 * VS].rearrange(
            "p (c j w) -> p c j w", c=KC, j=T1) for m in (Ms, Ns)]
        om = o_n[:, :, 0:NQ]
        wqs = stage[:, :, :].rearrange("p a n -> p (a n)").bitcast(BF16)[:, 0:2 * T1 * 112].rearrange(
            "p (a j m) -> p a j m", a=2, j=T1)
        aT = xn[:, :]
        mask_i = pr32[0:NQ, 0:NK].bitcast(I32)

        r_dram = nc.dram_tensor("r_rows", [NB, H, NQ], F32, kind="Internal").ap()

        k_dram = nc.dram_tensor("k_rows", [P, 2, NK], BF16, kind="Internal").ap()

        ps = stack.enter_context(nc.psum_tensor("ps", [P, 8 * 512], F32))

        def bank(k, n=512, p=P):
            return ps[0:p, k * 512:k * 512 + n]

        block = stack.enter_context(nc.Block())

        def fold_part(dst, a, g):
            v = dst[:, a, :].rearrange("p (a c s n) -> p a c s n", a=2, s=2, n=C)
            return v[:, g % 4 // 2, :, g % 2, :]

        BQ, BK, BV, BO, OB = 0, 8, 16, 24, 25

        def blocks_of(name, n, width=P):
            return [raw[name][:, width * k:width * (k + 1)] for k in range(n)]

        groups = []
        for g in range(2):
            n = 4 - g
            groups.append(("ld_x", blocks_of("x", 7)[4 * g:4 * g + n], P, xT[:, 512 * g:512 * g + P * n], None, 0))
        for name, dst in (("Wq", WqT), ("Wk", WkT), ("Wv", WvT)):
            for g in range(2):
                groups.append((f"ld_{name}", blocks_of(name, 8)[4 * g:4 * g + 4], P,
                               dst[:, 4 * g:4 * g + 4, :], None, 0))
        for g in range(E):
            groups.append(("ld_V1", blocks_of("V1", 32)[4 * g:4 * g + 4], P, None, V1s, 512 * g))
        for g in range(4):
            groups.append(("ld_V2", blocks_of("V2", 16)[4 * g:4 * g + 4], P, None, V2s, 512 * g))
        for g in range(3):
            groups.append(("ld_cx", [cx[:, 0, C * k:C * (k + 1)] for k in range(4 * g, 4 * g + 4)], KP,
                           None, cT[:, 0, :, :], BANKK * g))
        groups.append(("ld_l1", [wl1[:, k, :] for k in range(4)], P, wl1T[:, :, :], None, 0))
        NG = len(groups)
        split_before = [sum(g[4] is not None for g in groups[:k]) for k in range(NG + 1)]

        def context_load(sp, b, parity):
            sp.dma_start(cx[:, parity, :], ctx_d[b].rearrange("(p c) d -> p (c d)", c=KC)).then_inc(sem("ld_cx"), 16)

        @block.sync
        def _(sp):
            sp.dma_start(raw["x"].rearrange("p (t c) -> p t c", c=C),
                         x.rearrange("b q c -> (b q) c").rearrange("(t p) c -> p t c", p=P)).then_inc(sem("ld_x"), 16)
            for name, w in (("Wq", Wq), ("Wk", Wk), ("Wv", Wv)):
                sp.dma_start(raw[name], w).then_inc(sem(f"ld_{name}"), 16)
            sp.dma_start(raw["Wo"].rearrange("p (j c) -> p j c", c=C),
                         Wo.rearrange("(j p) c -> p j c", p=P)).then_inc(sem("ld_Wo"), 16)
            sp.dma_start(raw["V1"].rearrange("p (k c) -> p k c", c=C),
                         V1.rearrange("e (k p) c -> p (e k) c", p=P)).then_inc(sem("ld_V1"), 16)
            sp.dma_start(raw["V2"].rearrange("p (e f) -> p e f", e=E),
                         V2.rearrange("e c f -> c e f")).then_inc(sem("ld_V2"), 16)
            context_load(sp, 0, 0)
            for k, w in enumerate((w_q, w_k, w_v, w_o)):
                sp.dma_start(wl1[:, k, :], w).then_inc(sem("ld_l1"), 16)
            sp.wait_ge(sem("r_rows"), 2)
            sp.dma_start(r_dram.rearrange("b h q -> h b q"),
                         rrow.rearrange("h (b q) -> h b q", q=NQ)).then_inc(sem("r_out"), 16)
            sp.wait_ge(sem("r_out"), 16)
            sp.dma_start(rtile[:, :], r_dram.rearrange("b h q -> (b h q)").rearrange("(t p) -> t p", p=P)
                         ).then_inc(sem("r_in"), 16)
            def pair(i):
                for m in range(2):
                    if not (isinstance(i, int) and i == 0 and m == 0):
                        sp.wait_ge(sem("a0_O"), PAIR * i + TILES * m)
                    context_load(sp, (2 * i + m + 1) % NB if isinstance(i, int) else 2 * i + (m + 1), (m + 1) % 2)
            first_loop_last(sp, NB // 2, pair)
            sp.wait_ge(sem("a0_T"), 3 * STEPS)
            sp.dma_start(mask_i, mask_d[0, 0]).then_inc(sem("ld_mask"), 16)
            sp.wait_ge(sem("a0_O"), STEPS)
            sp.dma_start(cx[:, 1, :], ctx_d[1].rearrange("(p c) d -> p (c d)", c=KC)).then_inc(sem("ldc1"), 16)
            sp.wait_ge(sem("x_2"), 2)
            sp.wait_ge(sem("mbias"), 1)
            for a in range(2):
                for r0, q0, nq in MASK_ROWS:
                    sp.dma_start(ks[r0:r0 + nq, a], mbias[q0:q0 + nq, :].unsqueeze(1).broadcast_to([nq, T1, NK])
                                 ).then_inc(sem(f"ks_fixed{a}"), 16)
                sp.dma_start(ks[SHIFT_ROW:SHIFT_ROW + 3, a], tail[:, :].unsqueeze(1).broadcast_to([3, T1, NK])
                             ).then_inc(sem(f"ks_fixed{a}"), 16)

            def stack_keys(parity, b):
                sp.dma_start(k_dram, kT[:, :, :]).then_inc(sem("k_out"), 16)
                sp.wait_ge(sem("k_out"), 16 * b + 16)
                for r0, part in zip(STACK, (0, 0, 1)):
                    sp.dma_start(ks[r0:r0 + W1T, parity, :, :], k_dram[:, part, :].rearrange("(j d) n -> d j n", d=W1T)
                                 ).then_inc(sem(f"ks{parity}"), 16)
            sp.wait_ge(sem("k0_lo"), 3)
            stack_keys(0, 0)

            def pair1(i):
                for m in range(2):
                    b = 2 * i + m
                    if not (isinstance(i, int) and b >= NB - 2):
                        least(sp, sem("p_lo"), 9 * b - 6)
                        sp.dma_start(cx[:, m, :], ctx_d[2 * i + (m + 2)].rearrange("(p c) d -> p (c d)", c=KC)
                                     ).then_inc(sem(f"ldc{m}"), 16)
                    if not (isinstance(i, int) and b == NB - 1):
                        sp.wait_ge(sem("p_lo"), 18 * i + (9 * m + 6))
                        stack_keys(1 - m, b + 1)
            first_loop_last(sp, NB // 2, pair1)
            sp.wait_ge(sem("out_rows"), 2)
            sp.dma_start(out.rearrange("b q c -> (b q) c").rearrange("(t p) c -> p t c", p=P),
                         xn[:, :].rearrange("p (t c) -> p t c", c=C)).then_inc(sem("stored"), 16)
            sp.wait_ge(sem("stored"), 16)

        @block.gpsimd
        def _(pool):
            chain = [0]

            def link(ins):
                chain[0] += 1
                ins.then_inc(sem("pool_chain"), 1)
                pool.wait_ge(sem("pool_chain"), chain[0])

            def small(dst, src, name="ld_small"):
                pool.dma_start(dst, src).then_inc(sem(name), 16)

            pool.memset(b1c[:, E * 4:], 0.0).then_inc(sem("b1_pad"), 1)
            link(pool.memset(bias_c[:, :], 0.0))
            with nc.allow_non_contiguous_dma("a few small columns"):
                for c0, b_ in ((BQ, bq), (BK, bk), (BV, bv)):
                    small(bias_c[:, c0:c0 + 8], b_.rearrange("(j p) -> p j", p=P))
                small(bias_c[:, BO:BO + 1], bo.rearrange("(p a) -> p a", a=1))
                small(gates[:, 0:2], g_xattn.rearrange("(a n) -> a n", a=1).broadcast_to([P, 2]))
                small(gates[:, 2:4], g_ffn.rearrange("(a n) -> a n", a=1).broadcast_to([P, 2]))
                small(wg_raw[:, :], Wg)
                small(Wr_T[:, :], Wr.rearrange("e c -> c e"))
                small(b1c[:, 0:E * 4], b1.rearrange("e (k p) -> p (e k)", p=P))
                small(b2c[:, :], b2.rearrange("e c -> c e"))
            link(pool.memset(ident[:, :], 0.0))
            pool.affine_select(out=ident[:, :], in_=ident[:, :], compare_op=ALU.not_equal, fill=1.0, base=0,
                               pattern=[[-1, P]], channel_multiplier=1).then_inc(sem("ident"), 1)
            pool.wait_ge(sem("ident"), 1)
            pool.tensor_copy(identb[:, :], ident[:, :])
            pool.memset(mean_w[:, :], 1.0 / C)
            pool.memset(eps_c[:, :], EPS)
            pool.memset(ones_c[:, :], 1.0)
            link(pool.memset(prod[:, :], 0.0))
            pool.memset(parity_c[:, :], 1.0)
            pool.memset(ones_q[:, :], 1.0)
            link(pool.memset(tril[:, :, :], 1.0))
            link(pool.memset(tail[:, :], 1.0))
            pool.memset(pick[:, :, :, :], 0.0)
            pool.memset(place_m[:, :], 0.0)
            link(pool.memset(block1[:, :], 1.0))
            link(pool.memset(rep[:, :], 0.0))
            blk = block1[:, :].rearrange("p (b j) -> p b j", j=16)
            link(pool.affine_select(out=blk, in_=blk, compare_op=ALU.is_ge, fill=0.0, base=0,
                                    pattern=[[-16, 8], [0, 16]], channel_multiplier=1))
            link(pool.affine_select(out=blk, in_=blk, compare_op=ALU.is_ge, fill=0.0, base=15,
                                    pattern=[[16, 8], [0, 16]], channel_multiplier=-1))
            for r0 in STACK:
                v = parity_c[r0:r0 + W1T, 0:1]
                link(pool.affine_select(out=v, in_=v, compare_op=ALU.is_ge, fill=0.0, base=DH1 - 1,
                                        pattern=[[0, 1]], channel_multiplier=-1))
                v = parity_c[r0:r0 + W1T, 1:2]
                link(pool.affine_select(out=v, in_=v, compare_op=ALU.is_ge, fill=0.0, base=-DH1,
                                        pattern=[[0, 1]], channel_multiplier=1))
            for s_ in range(2):
                for kind, rows in enumerate(((DH1 * s_, W1T + 1 + DH1 * s_), (W1T,))):
                    v = pick[:, kind, s_, 96:128].rearrange("p (j x) -> p j x", x=W1T)[:, :, DH1 * s_:DH1 * (s_ + 1)]
                    for row in rows:
                        link(pool.affine_select(out=v, in_=v, compare_op=ALU.not_equal, fill=1.0, base=-row,
                                                pattern=[[-64, 2], [0 if kind else -1, DH1]], channel_multiplier=1))
            for r0, q0, nq in MASK_ROWS:
                v = place_m[:, r0:r0 + nq]
                link(pool.affine_select(out=v, in_=v, compare_op=ALU.not_equal, fill=1.0, base=-q0,
                                        pattern=[[-1, nq]], channel_multiplier=1))
            link(pool.affine_select(out=tril[:, :, :], in_=tril[:, :, :], compare_op=ALU.is_ge, fill=0.0, base=-1,
                                    pattern=[[1, E], [-1, E]], channel_multiplier=0))
            rep3 = rep[:, :].rearrange("j (b q) -> j b q", q=NQ)
            link(pool.affine_select(out=rep3, in_=rep3, compare_op=ALU.not_equal, fill=1.0, base=0,
                                    pattern=[[0, NB // 2], [-1, NQ]], channel_multiplier=1))
            for r, s in enumerate(SHIFTS):
                pool.memset(powc[:, r:r + 1], float(2 ** s))
            pool.memset(valid[:, 0:7], 1.0)
            pool.iota(pj[:, :], pattern=[[0, 16]], base=0, channel_multiplier=1).then_inc(sem("consts"), 1)

            pool.wait_ge(sem("folds0"), 8)

            def split_expert(e):
                least(pool, sem("w_lo"), 2 * e)
                apart(pool, sem("ident"))
                for k, (w, ws) in enumerate(((W1[e], W1s), (W2[e].rearrange("(k p) c -> p k c", p=P), W2s))):
                    dst = stage[:, k, :]
                    if k:
                        dst = dst.rearrange("p (k c) -> p k c", c=C)
                    pool.dma_start(dst, w).then_inc(sem(f"ld_stage{k}"), 16)
                for k, ws in enumerate((W1s, W2s)):
                    pool.wait_ge(sem(f"ld_stage{k}"), 16 * (e + 1))
                    pool.tensor_copy(ws[:, 0, bass.ds(e * FF0, FF0)], stage[:, k, :]).then_inc(sem("w_hi"), 1)
                    pool.wait_ge(sem("w_hi"), 2 * e + (k + 1))
                    pool.tensor_tensor(ws[:, 1, bass.ds(e * FF0, FF0)], stage[:, k, :],
                                       ws[:, 0, bass.ds(e * FF0, FF0)], ALU.subtract).then_inc(sem("w_lo"), 1)
            first_loop_last(pool, E, split_expert)

            pool.wait_ge(sem("prep_a"), NG)
            pool.wait_ge(sem("w_lo"), 2 * E)
            link(pool.tensor_copy(kvs[:, 0], wl1T[:, 1:3, :]))
            link(pool.tensor_tensor(kvs[:, 1], wl1T[:, 1:3, :], kvs[:, 0], ALU.subtract))
            link(pool.memset(wqs, 0.0))
            link(pool.tensor_scalar(wl1T[:, 0, :], wl1T[:, 0, :], DH1 ** -0.5, None, ALU.mult))
            wq3 = wl1T[:, 0, :].rearrange("p (j d) -> p j d", d=W1T)
            for r0 in STACK:
                v = lambda a: wqs[:, a, :, r0:r0 + W1T]
                link(pool.tensor_copy(v(0), wq3))
                link(pool.tensor_tensor(v(1), wq3, v(0), ALU.subtract))
            pool.sem_inc(sem("w1_ready"), 1)

            def hidden_lows(L, units):
                def lows(e):
                    for k in range(units):
                        pool.wait_ge(sem(f"f{L}_hi"), units * e + (k + 1))
                        pool.tensor_tensor(hid_s[:, 1, k % 4, :], hid[:, k % 4, :], hid_s[:, 0, k % 4, :],
                                           ALU.subtract).then_inc(sem(f"f{L}_lo"), 1)
                first_loop_last(pool, E, lows)
            hidden_lows(0, 8)

            def prob_lows(i):
                for n in range(2 * T1):
                    for g in range(3):
                        pool.wait_ge(sem("b_E"), 6 * T1 * i + (3 * n + g + 1))
                        part = slice(4 * R1 * g, 4 * R1 * (g + 1))
                        pool.tensor_tensor(p_s[:, n % 2, 1, part], p_f[:, part], p_s[:, n % 2, 0, part], ALU.subtract
                                           ).then_inc(sem("b_lo"), 1)
            first_loop_last(pool, NB // 2, prob_lows)
            hidden_lows(1, 4)

        def head_view(a, h, half):
            v = qo[:, a, :].rearrange("c (b h q) -> c b h q", h=H, q=NQ)
            return v[:, 8 * half:8 * half + 8, h, :]

        def three(pe, dst, w, m, start=True, stop=True):
            pe.matmul(dst, w(0), m(0), start=start, stop=False, skip_group_check=True)
            pe.matmul(dst, w(0), m(1), start=False, stop=False, skip_group_check=True)
            return pe.matmul(dst, w(1), m(0), start=False, stop=stop, skip_group_check=True)

        def pe_norm(pe, k):
            for h in range(2):
                if k:
                    pe.wait_ge(sem(f"x_{k}"), h + 1)
                pe.matmul(bank(h, HALF), mean_w[:, :], xT[:, HALF * h:HALF * (h + 1)],
                          start=True, stop=True).then_inc(sem("n_mean"), 1)
            for h in range(2):
                pe.wait_ge(sem("n_sq"), 2 * k + h + 1)
                pe.matmul(bank(2 + h, HALF), mean_w[:, :], sq[:, HALF * h:HALF * (h + 1)],
                          start=True, stop=True).then_inc(sem("n_var"), 1)

        def pe_fold_queries(pe, L):
            pe.wait_ge(sem("n_lo"), 2)
            pe.wait_ge(sem("M0"), 4)

            def two_heads(i):
                for k in range(4):
                    h, half = 2 * i + k // 2, k % 2
                    least(pe, sem(f"q{L}_lo"), 4 * i + (k - 3))
                    three(pe, bank(4 + k, HALF), lambda a: Ms[:, a, bass.ds(h * C, C)],
                          lambda a: xn_s[:, a, HALF * half:HALF * (half + 1)]).then_inc(sem(f"q{L}"), 1)
            first_loop_last(pe, H // 2, two_heads)

        def scores_bank(pe, L, s, n, j):
            parity = (n // TILES) % 2
            for k, (a, b) in enumerate(((0, 0), (0, 1), (1, 0))):
                last = pe.matmul(bank(j, BANKK), qo[:, a, bass.ds(s * P, P)], cT[:, parity, b, BANKK * j:BANKK * (j + 1)],
                                 start=k == 0, stop=k == 2)
            last.then_inc(sem(f"a{L}_S"), 1)

        def pe_step(pe, L, i, n):
            s = PAIR * i + n
            t, parity = n % TILES, (n // TILES) % 2
            final = isinstance(s, int) and s == STEPS - 1
            initial = isinstance(s, int) and s == 0
            for j in range(3):
                pe.wait_ge(sem(f"a{L}_E"), 3 * s + (j + 1))
                if not final:
                    if j == 0 and n % TILES == TILES - 1:
                        pe.wait_ge(sem(f"cT{L}"), 4 * (2 * i + (n // TILES + 1)))
                    scores_bank(pe, L, s + 1, (n + 1) % PAIR, j)
                if j == 0 and not initial:
                    pe.wait_ge(sem(f"a{L}_pTd"), 2 * s)
                    pe.wait_ge(sem(f"a{L}_pTa"), s)
                for c in range(4):
                    k = 4 * j + c
                    last = pe.transpose(bank(3 + j)[0:KP, c * P:(c + 1) * P], pr[:, n % 2, k * KP:(k + 1) * KP], ident[:, :])
                last.then_inc(sem(f"a{L}_T"), 1)
            if not initial:
                pe.wait_ge(sem(f"a{L}_on"), s)
                if 2 <= t <= 5 and not (L == 1 and isinstance(i, int) and i == NB // 2 - 1 and n >= TILES):
                    if t == 2:
                        b1_ = 2 * i + (n // TILES + 1)
                        pe.wait_ge(sem("ld_cx"), 16 * (16 * L + 1) + 16 * b1_)
                    for c in range(3):
                        k = 3 * (t - 2) + c
                        pe.transpose(bank(6 + (n + 1) % 2)[:, c * KP:(c + 1) * KP],
                                     cx[:, 1 - parity, k * C:(k + 1) * C], ident[0:KP, 0:KP])
                pe.transpose(bank(6 + (n + 1) % 2)[:, 384:512], o_n[:, (n + 1) % 2, :], ident[:, :]
                             ).then_inc(sem(f"a{L}_OT"), 1)
            if isinstance(s, int):
                least(pe, sem(f"a{L}_olo"), s - 1)
            else:
                pe.wait_ge(sem(f"a{L}_olo"), s - 1)
            for k in range(KC):
                if k == 0:
                    pe.wait_ge(sem(f"a{L}_pTd"), 2 * s + 1)
                if k == 4:
                    pe.wait_ge(sem(f"a{L}_pTa"), s + 1)
                if k == 8:
                    pe.wait_ge(sem(f"a{L}_pTd"), 2 * s + 2)
                last = pe.matmul(bank(6 + n % 2)[:, 384:512], pT[:, k * P:(k + 1) * P], cx[:, parity, k * C:(k + 1) * C],
                                 start=k == 0, stop=k == KC - 1)
            last.then_inc(sem(f"a{L}_O"), 1)

        def pe_attention(pe, L):
            pe.wait_ge(sem(f"q{L}_lo"), 2 * H)
            for j in range(3):
                scores_bank(pe, L, 0, 0, j)

            def pair(i):
                for n in range(PAIR):
                    pe_step(pe, L, i, n)
            first_loop_last(pe, NB // 2, pair)
            pe.wait_ge(sem(f"a{L}_on"), STEPS)
            pe.transpose(bank(6 + (STEPS - 1) % 2)[:, 384:512], o_n[:, (STEPS - 1) % 2, :], ident[:, :]
                         ).then_inc(sem(f"a{L}_OT"), 1)

        def keys_mm(pe, dst, parity, g):
            return three(pe, dst, lambda a: kvs[:, a, 0, :], lambda a: cT[:, parity, a, BANKK * g:BANKK * (g + 1)])

        def values_mm(pe, dst, parity, g):
            for c in range(4):
                k = 4 * g + c
                last = three(pe, dst[0:KP, C * c:C * (c + 1)], lambda a: cT[:, parity, a, KP * k:KP * (k + 1)],
                             lambda a: kvs[:, a, 1, :])
            return last

        def pe_stack_queries(pe):
            pe.wait_ge(sem("n_lo"), 6)

            def two_tiles(i):
                for k in range(4):
                    j, half = 2 * i + k // 2, k % 2
                    least(pe, sem("qs_lo"), 4 * i + (k - 3))
                    dst = bank(4 + k, HALF, KS_ROWS)
                    three(pe, dst, lambda a: wqs[:, a, j, 0:KS_ROWS] if isinstance(j, int) else
                          wqs[:, a].rearrange("p j m -> p (j m)")[:, bass.ds(j * 112, KS_ROWS)],
                          lambda a: xn_s[:, a, HALF * half:HALF * (half + 1)], stop=False)
                    pe.matmul(dst, place_m[:, 0:KS_ROWS], rep[:, :], start=False, stop=True, skip_group_check=True
                              ).then_inc(sem("qs_mm"), 1)
            first_loop_last(pe, T1 // 2, two_tiles)

        def tile_scores(pe, tau, n):
            j, parity = n % T1, n // T1 % 2
            for g in range(3):
                last = pe.matmul(bank(g, BANKK, R1), qs[0:KS_ROWS, bass.ds(tau * R1, R1)],
                                 ks[0:KS_ROWS, parity, j, BANKK * g:BANKK * (g + 1)], start=True, stop=True)
                if g:
                    last.then_inc(sem("b_Sq"), 1)

        def merged(kind):
            return bank(3 + kind)[:, 4 * R1:4 * R1 + NQ]

        def ahead(i, n, d):
            return not (isinstance(i, int) and 2 * T1 * i + n + d >= STEPS1)

        def preparation(i, n):
            m = n // T1 + (n % T1 >= PARTS.index((0,)))
            b = 2 * i + m
            return b, 1 - m % 2, () if isinstance(i, int) and b >= NB - 1 else PARTS[n % T1]

        def next_item(pe, i, n, k):
            b, par, _ = preparation(i, n)
            if k == 0:
                least(pe, sem("p_lo"), 9 * b)
                pe.wait_ge(sem(f"ldc{par}"), 16 * i + 16 * (1 + (n + 2) // (2 * T1)))
            else:
                pe.wait_ge(sem("p_lo"), 9 * b + k)
            if k < 3:
                for c in range(4):
                    last = pe.transpose(bank(7)[:, KP * c:KP * (c + 1)], cx[:, par, C * (4 * k + c):C * (4 * k + c + 1)],
                                        ident[0:KP, 0:KP])
            elif k < 6:
                last = keys_mm(pe, bank(7, BANKK), 0, k - 3)
            else:
                last = values_mm(pe, bank(7), 0, k - 6)
            last.then_inc(sem("p_mm"), 1)

        def pe_step1(pe, i, n):
            tau = 2 * T1 * i + n
            j, b = n % T1, 2 * i + n // T1
            parts = preparation(i, n)[2]
            if ahead(i, n, 2):
                pe.wait_ge(sem("b_m"), tau + 2)
                if j == T1 - 2:
                    pe.wait_ge(sem(f"ks{1 - n // T1}"), KS_LOADS * (i + n // T1) + KS_LOADS)
                tile_scores(pe, tau + 2, (n + 2) % (2 * T1))
            for k in parts[:-1]:
                next_item(pe, i, n, k)
            if j - 1 in MERGE and not (isinstance(b, int) and b == 0):
                pe.wait_ge(sem("om_cp"), 2 * b + (MERGE.index(j - 1) - 1))
            for g in range(3):
                least(pe, sem("b_E"), 3 * tau + (g - 2))
                if g == 0:
                    pe.wait_ge(sem("b_sh"), tau + 1)
                if g == 2 and ahead(i, n, 1):
                    shift(pe, tau + 1, n + 1)
                for c in range(4):
                    k = 4 * g + c
                    last = pe.matmul(bank(3 + g)[0:KP, R1 * c:R1 * (c + 1)], ks[0:KS_ROWS, n // T1, j, KP * k:KP * (k + 1)],
                                     qs[0:KS_ROWS, bass.ds(tau * R1, R1)], start=True, stop=True)
                last.then_inc(sem("b_St"), 1)
            if len(parts) == 1:
                next_item(pe, i, n, parts[0])
            if not (isinstance(tau, int) and tau == 0):
                outputs(pe, i, n)
            if len(parts) == 2:
                next_item(pe, i, n, parts[1])
            if j in MERGE and not (isinstance(b, int) and b == 0):
                kind = MERGE.index(j)
                pe.wait_ge(sem("b_E"), 3 * tau + (kind + 1))
                merge_outputs(pe, b, 1 - n // T1, kind)

        def shift(pe, tau, n):
            pe.wait_ge(sem("b_h"), tau + 1)
            pe.transpose(bank(5)[0:2, 4 * R1:4 * R1 + R1 // 2].bitcast(BF16), mh[:, n % 2, :], identb[0:R1, 0:R1]
                         ).then_inc(sem("b_shT"), 1)

        def outputs(pe, i, n):
            tau = 2 * T1 * i + n
            t = (n - 1) % (2 * T1)
            j, par = t % T1, t // T1
            least(pe, sem("b_ev"), tau - 1)
            if j == 0:
                least(pe, sem("p_lo"), 9 * (2 * i + n // T1))
            for a, ready in ((0, "b_E"), (1, "b_lo")):
                pe.wait_ge(sem(ready), 3 * tau)
                for k in range(KC):
                    last = pe.matmul(bank(6, R1, VW), vals[par][:, k, j, 0:VW], p_s[:, t % 2, a, R1 * k:R1 * (k + 1)],
                                     start=a + k == 0, stop=a + k == KC)
            last.then_inc(sem("b_O"), 1)

        def merge_outputs(pe, b, par, kind):
            pe.wait_ge(sem("b_ev"), T1 * b)
            for g in range(4):
                for s_ in range(2):
                    last = pe.matmul(merged(kind), pick[:, kind, s_, 32 * (3 - g):32 * (3 - g) + P],
                                     o1[:, par, g, NQ * s_:NQ * (s_ + 1)], start=g + s_ == 0, stop=g + s_ == 4)
            last.then_inc(sem("om_mm"), 1)

        def pe_attention1(pe):
            pe.wait_ge(sem("qs_lo"), 2 * T1)
            pe.wait_ge(sem("v_ones"), 1)
            for a in range(2):
                pe.wait_ge(sem(f"ks_fixed{a}"), 80)
            pe.wait_ge(sem("ks0"), KS_LOADS)
            tile_scores(pe, 0, 0)
            next_item(pe, -1, 2 * T1 - 2, 0)
            pe.wait_ge(sem("b_m"), 1)
            tile_scores(pe, 1, 1)
            shift(pe, 0, 0)
            next_item(pe, -1, 2 * T1 - 1, 1)

            def pair(i):
                for n in range(2 * T1):
                    pe_step1(pe, i, n)
            first_loop_last(pe, NB // 2, pair)
            outputs(pe, NB // 2, 0)
            pe.wait_ge(sem("b_E"), 3 * STEPS1)
            for kind in range(2):
                merge_outputs(pe, NB, 1, kind)

        def pe_project(pe, L):
            pe.wait_ge(sem(f"a{L}_olo"), STEPS)
            pe.wait_ge(sem("N0"), 4)
            for half in range(2):
                for h in range(H):
                    last = three(pe, bank(4 + half, HALF).rearrange("p (b q) -> p b q", q=NQ), lambda a: Ns[:, a, h * C:(h + 1) * C],
                                 lambda a: head_view(a, h, half), start=h == 0, stop=h == H - 1)
                last.then_inc(sem(f"proj{L}"), 1)

        def pe_experts(pe, L):
            units = 8 if L == 0 else 4
            pe.wait_ge(sem("n_lo"), 4 * L + 4)

            def up(e, v):
                k = v % units
                de = v // units
                f, half = k // 2, k % 2
                m = lambda a: xn_s[:, a, HALF * half:HALF * (half + 1)]
                if L == 0:
                    least(pe, sem("f0_h"), 8 * e + (v - 3))
                    last = three(pe, bank(2 + k % 4, HALF), lambda a: W1s[:, a, bass.ds(e * FF0 + (de * FF0 + f * P), P)], m)
                else:
                    least(pe, sem("f1_h"), 4 * e + (v - 1))
                    three(pe, bank(4 + k % 2, HALF), lambda a: V1s[:, a, bass.ds(e * 512 + (de * 512 + FF1 + f * P), P)], m)
                    last = three(pe, bank(2 + k % 2, HALF), lambda a: V1s[:, a, bass.ds(e * 512 + (de * 512 + f * P), P)], m)
                last.then_inc(sem(f"f{L}_up"), 1)

            def expert(e):
                for k in range(units):
                    if not (isinstance(e, int) and e == E - 1 and k >= units - 2):
                        up(e, k + 2)
                    pe.wait_ge(sem(f"f{L}_lo"), units * e + (k + 1))
                    f, half = k // 2, k % 2
                    if f == 0:
                        least(pe, sem(f"f{L}_y"), 2 * e + (half - 1))
                    ws, width = (W2s, FF0) if L == 0 else (V2s, FF1)
                    three(pe, bank(6 + half, HALF), lambda a: ws[:, a, bass.ds(e * width + f * P, P)],
                          lambda a: hid_s[:, a, k % 4, :], start=f == 0, stop=f == units // 2 - 1
                          ).then_inc(sem(f"f{L}_Y"), 1)
                    if L == 0 and k == 4:
                        pe.wait_ge(sem("tk_flag"), e + 1)
                        pe.matmul(bank(0, 1), block1[:, :], flag[:, 0:1], start=True, stop=True).then_inc(sem("tk_sum"), 1)
            if L == 0:
                pe.wait_ge(sem("w_lo"), 2 * E)
            up(0, 0)
            up(0, 1)
            first_loop_last(pe, E, expert)
            pe.wait_ge(sem(f"g{L}"), 1)
            for e in range(E):
                for half in range(2):
                    k = 2 * e + half
                    least(pe, sem(f"c{L}"), k - 1)
                    w = (ident[:, 16 * e:16 * e + 1] if L == 0 else ident[0:E, e:e + 1]).broadcast_to([P if L == 0 else E, P])
                    m = sel[:, HALF * half:HALF * (half + 1)] if L == 0 else sel[0:E, HALF * half:HALF * (half + 1)]
                    pe.matmul(bank(half, HALF), w, m, start=True, stop=True).then_inc(sem(f"gb{L}"), 1)

        @block.tensor
        def _(pe):
            pe.wait_ge(sem("ident"), 1)
            for k, (load, srcs, rows, f32, split, col) in enumerate(groups):
                pe.wait_ge(sem(load), 64 if load == "ld_l1" else 16)
                if k >= 8:
                    pe.wait_ge(sem("prep_a"), k - 7)
                    if groups[k - 8][4] is not None:
                        pe.wait_ge(sem("prep_d"), split_before[k - 7])
                for c, src in enumerate(srcs):
                    last = pe.transpose(bank(k % 8)[:, c * rows:(c + 1) * rows], src, ident[0:rows, 0:rows])
                last.then_inc(sem("prep"), 1)
            pe.wait_ge(sem("prep_a"), NG)
            pe.wait_ge(sem("prep_d"), split_before[NG])
            pe.wait_ge(sem("ld_Wo"), 16)
            for g in range(8):
                wl, wr = (WqT, WkT) if g < 4 else (WvT, raw["Wo"].rearrange("p (j c) -> p j c", c=C))
                for c in range(4):
                    h = 8 * (g % 4 // 2) + 2 * c + g % 2
                    r = slice(64 * (h % 2), 64 * (h % 2) + 64)
                    last = pe.matmul(bank(g)[:, c * C:(c + 1) * C], wl[r, h // 2, :], wr[r, h // 2, :], start=True, stop=True)
                last.then_inc(sem("fold_mm"), 1)
            pe.wait_ge(sem("M0"), 4)
            pe.wait_ge(sem("ld_small"), 160)
            pe.wait_ge(sem("prod"), 2)
            for h in range(H):
                r = slice(64 * (h % 2), 64 * (h % 2) + 64)
                pe.matmul(bank(h % 2)[:, h:h + 1], WkT[r, h // 2, :], bias_c[r, BQ + h // 2:BQ + h // 2 + 1], start=True, stop=True)
                pe.matmul(bank(h % 2)[:, 16 + h:17 + h], WqT[r, h // 2, :], bias_c[r, BK + h // 2:BK + h // 2 + 1], start=True, stop=True)
            for j in range(8):
                pe.matmul(bank(0)[:, 32:33], raw["Wo"][:, C * j:C * (j + 1)], bias_c[:, BV + j:BV + j + 1],
                          start=j == 0, stop=j == 7)
            pe.wait_ge(sem("consts"), 1)
            pe.matmul(bank(0)[0:H, 33:34], prod[:, :], ones_c[:, :], start=True, stop=True).then_inc(sem("bias_mm"), 1)
            pe.wait_ge(sem("bias_cols"), 1)
            pe_norm(pe, 0)
            pe.wait_ge(sem("n_lo"), 2)
            for half in range(2):
                pe.matmul(bank(half, HALF, H), U[:, :], xn[:, HALF * half:HALF * (half + 1)],
                          start=True, stop=True).then_inc(sem("r_mm"), 1)
            pe_fold_queries(pe, 0)
            pe.wait_ge(sem("r_in"), 16)
            pe.wait_ge(sem("r_rows"), 2)
            pe.transpose(bank(0)[:, 0:STEPS], rtile[:, :], ident[0:STEPS, 0:STEPS]).then_inc(sem("r_T"), 1)
            pe.wait_ge(sem("rcol"), 1)
            pe_attention(pe, 0)
            pe_project(pe, 0)
            pe_norm(pe, 1)
            pe.wait_ge(sem("n_lo"), 4)
            for half in range(2):
                pe.matmul(bank(half, HALF), Wg_rep[:, :, :].rearrange("p e j -> p (e j)"),
                          xn[:, HALF * half:HALF * (half + 1)], start=True, stop=True).then_inc(sem("z"), 1)
            pe_experts(pe, 0)
            pe.wait_ge(sem("x_2"), 2)
            pe.wait_ge(sem("w1_ready"), 1)
            for g in range(3):
                keys_mm(pe, bank(g, BANKK), 0, g).then_inc(sem("k0_mm"), 1)
            for g in range(3):
                values_mm(pe, bank(3 + g), 0, g).then_inc(sem("v0_mm"), 1)
            pe.wait_ge(sem("repk"), 1)
            pe.matmul(bank(6, HALF), ones_q[:, :], repk[:, :], start=True, stop=True).then_inc(sem("keep_mm"), 1)
            pe.wait_ge(sem("k0_lo"), 3)
            pe.wait_ge(sem("v0_lo"), 3)
            pe_norm(pe, 2)
            pe_stack_queries(pe)
            pe_attention1(pe)
            pe.wait_ge(sem("om_done"), NB)
            for half in range(2):
                pe.matmul(bank(4 + half, HALF), woT, aT[:, HALF * half:HALF * (half + 1)], start=True, stop=True
                          ).then_inc(sem("proj1"), 1)
            pe_norm(pe, 3)
            pe.wait_ge(sem("n_lo"), 8)
            for t in range(7):
                last = pe.matmul(bank(0)[:, E * t:E * (t + 1)], xn[:, P * t:P * (t + 1)], Wr_T[:, :], start=True, stop=True)
            last.then_inc(sem("lg"), 1)
            pe.wait_ge(sem("rw"), 1)
            for t in range(7):
                last = pe.transpose(bank(t // 4)[0:E, P * (t % 4):P * (t % 4 + 1)], tmp[:, E * t:E * (t + 1)], ident[:, :])
            last.then_inc(sem("rw_T"), 1)
            pe.wait_ge(sem("g1"), 1)
            pe_experts(pe, 1)
            pe.wait_ge(sem("x_4"), 2)
            for t in range(7):
                last = pe.transpose(bank(t // 4)[:, P * (t % 4):P * (t % 4 + 1)], xT[:, P * t:P * (t + 1)], ident[:, :])
                if t in (3, 6):
                    last.then_inc(sem("xT_rows"), 1)

        def act_norm(act, k):
            for h in range(2):
                act.wait_ge(sem("n_var"), 2 * k + h + 1)
                act.activation(sq[:, HALF * h:HALF * (h + 1)], bank(2 + h, HALF), ACT.Sqrt, bias=eps_c[:, :]
                               ).then_inc(sem("n_sd"), 1)
            for h in range(2):
                act.wait_ge(sem("n_xn"), 2 * k + h + 1)
                act.activation(xn_s[:, 0, HALF * h:HALF * (h + 1)], xn[:, HALF * h:HALF * (h + 1)], ACT.Copy
                               ).then_inc(sem("n_hi"), 1)

        def act_fold_queries(act, L):
            def two_heads(i):
                for k in range(4):
                    h, half = 2 * i + k // 2, k % 2
                    act.wait_ge(sem(f"q{L}"), 4 * i + (k + 1))
                    apart(act, sem("prep"))
                    act.activation(head_view(0, h, half) if isinstance(h, int) else dyn_head(0, h, half),
                                   bank(4 + k, HALF).rearrange("p (b q) -> p b q", q=NQ),
                                   ACT.Identity, bias=qbias[:, bass.ds(h, 1)]).then_inc(sem(f"q{L}_hi"), 1)
            first_loop_last(act, H // 2, two_heads)

        def dyn_head(a, h, half):
            v = qo[:, a, :].rearrange("c (b n) -> c b n", n=H * NQ)
            return v[:, 8 * half:8 * half + 8, bass.ds(h * NQ, NQ)]

        def act_exp(act, L, s, n):
            act.wait_ge(sem(f"a{L}_nb"), s + 1)
            for j in range(3):
                act.activation(pr[:, n % 2, BANKK * j:BANKK * (j + 1)], bank(j, BANKK), ACT.Exp, bias=nb[:, n % 2:n % 2 + 1],
                               accum_out=sums[:, n % 2, j:j + 1]).then_inc(sem(f"a{L}_E"), 1)

        def context_share(L, i, n):
            t = n % TILES
            if not 2 <= t <= 5 or (L == 1 and isinstance(i, int) and i == NB // 2 - 1 and n >= TILES):
                return None
            return 1 - (n // TILES) % 2, 3 * KP * (t - 2)

        def act_out_hi(act, L, i, n):
            s = PAIR * i + n
            act.wait_ge(sem(f"a{L}_OT"), s)
            b = bank(6 + (n + 1) % 2)
            share = context_share(L, i, n)
            if share:
                act.activation(cT[:, share[0], 0, share[1]:share[1] + 3 * KP], b[:, 0:3 * KP], ACT.Copy)
            else:
                apart(act, sem("prep"))
            act.activation(qo[:, 0, bass.ds(s * P - P, P)], b[:, 384:512], ACT.Copy).then_inc(sem(f"a{L}_ohi"), 1)

        def act_attention(act, L):
            act_exp(act, L, 0, 0)

            def pair(i):
                for n in range(PAIR):
                    s = PAIR * i + n
                    act.wait_ge(sem(f"a{L}_T"), 3 * s + 2)
                    act.activation(pT[:, 4 * P:8 * P], bank(4)[0:KP, :], ACT.Copy).then_inc(sem(f"a{L}_pTa"), 1)
                    if not (isinstance(s, int) and s == 0):
                        act_out_hi(act, L, i, n)
                    if not (isinstance(s, int) and s == STEPS - 1):
                        act_exp(act, L, s + 1, (n + 1) % PAIR)
                    act.wait_ge(sem(f"a{L}_O"), s + 1)
                    act.wait_ge(sem(f"a{L}_rd"), s + 1)
                    act.activation(o_n[:, n % 2, :], bank(6 + n % 2)[:, 384:512], ACT.Copy, scale=den[:, n % 2:n % 2 + 1]
                                   ).then_inc(sem(f"a{L}_on"), 1)
            first_loop_last(act, NB // 2, pair)
            act.wait_ge(sem(f"a{L}_OT"), STEPS)
            act.activation(qo[:, 0, (STEPS - 1) * P:STEPS * P], bank(6 + (STEPS - 1) % 2)[:, 384:512], ACT.Copy
                           ).then_inc(sem(f"a{L}_ohi"), 1)

        shift_rows = bank(5)[0:2, 4 * R1:4 * R1 + R1 // 2].bitcast(BF16)

        def qs_part(r0, r1, j, half, s_):
            v = qs[r0:r1].rearrange("p (b n) -> p b n", n=T1 * R1)
            return v[:, 8 * half:8 * half + 8, bass.ds(j * R1 + s_ * NQ, NQ)]

        def act_values(act, parity, g, k, done):
            act.activation(vals[parity][:, 4 * g:4 * g + 4, :, 0:W1T],
                           bank(k)[0:KP, :].rearrange("p (c j d) -> p c j d", c=4, j=T1), ACT.Copy).then_inc(sem(done), 1)

        def act_experts(act, L):
            units = 8 if L == 0 else 4

            def hidden(e, v):
                k, de = v % units, v // units
                f, half = k // 2, k % 2
                act.wait_ge(sem(f"f{L}_up"), units * e + (v + 1))
                if L == 0:
                    act.activation(hid[:, k % 4, :], bank(2 + k % 4, HALF), ACT.Gelu,
                                   bias=b1_now[:, 4 * de + f:4 * de + f + 1]).then_inc(sem("f0_h"), 1)
                else:
                    least(act, sem("f1_h"), 4 * e + (v - 1))
                    act.activation(sel_silu(k % 2), bank(4 + k % 2, HALF), ACT.Silu).then_inc(sem("f1_silu"), 1)

            def biases(e):
                act.wait_ge(sem("b1_now"), e + 1)

            def expert(e):
                if L == 0 and not (isinstance(e, int) and e == 0):
                    biases(e)
                for k in range(units):
                    if not (isinstance(e, int) and e == E - 1 and k >= units - 2):
                        hidden(e, k + 2)
                    if k >= units - 2:
                        half = k % 2
                        act.wait_ge(sem(f"f{L}_Y"), units * e + (k + 1))
                        apart(act, sem("prep"))
                        if L == 0:
                            act.activation(y_e[:, bass.ds(e * TOK + HALF * half, HALF)], bank(6 + half, HALF), ACT.Identity,
                                           bias=b2c[:, bass.ds(e, 1)]).then_inc(sem("f0_y"), 1)
                        else:
                            act.activation(y_e[:, bass.ds(e * TOK + HALF * half, HALF)], bank(6 + half, HALF), ACT.Copy
                                           ).then_inc(sem("f1_y"), 1)
            if L == 0:
                biases(0)
            hidden(0, 0)
            hidden(0, 1)
            first_loop_last(act, E, expert)

        def sel_silu(k):
            return sq[:, HALF * k:HALF * (k + 1)]

        def half_of(t, h):
            return t[:, HALF * h:HALF * (h + 1)]

        @block.scalar
        def _(act):
            for k, (load, srcs, rows, f32, split, col) in enumerate(groups):
                act.wait_ge(sem("prep"), k + 1)
                n = rows * len(srcs)
                src = bank(k % 8, n)
                if f32 is not None:
                    if len(f32.shape) == 3:
                        src = src.rearrange("p (j c) -> p j c", c=C)
                    act.activation(f32, src, ACT.Copy).then_inc(sem("prep_a"), 1)
                else:
                    act.activation(split[:, 0, col:col + n], src, ACT.Copy).then_inc(sem("prep_a"), 1)
            for g in range(8):
                act.wait_ge(sem("fold_mm"), g + 1)
                dst, scale = (Ms, DH0 ** -0.5) if g < 4 else (Ns, 1.0)
                act.activation(fold_part(dst, 0, g), bank(g).rearrange("p (c n) -> p c n", n=C), ACT.Copy, scale=scale
                               ).then_inc(sem("fold_hi"), 1)
            act.wait_ge(sem("ld_small"), 160)
            act.wait_ge(sem("b1_pad"), 1)
            act.activation(gates[:, :], gates[:, :], ACT.Tanh).then_inc(sem("tanh"), 1)
            act_norm(act, 0)
            for half in range(2):
                act.wait_ge(sem("r_mm"), half + 1)
                act.wait_ge(sem("bias_cols"), 1)
                act.activation(rrow[:, HALF * half:HALF * (half + 1)], bank(half, HALF, H), ACT.Identity, bias=crow[:, :]
                               ).then_inc(sem("r_rows"), 1)
            act_fold_queries(act, 0)
            act_attention(act, 0)
            act_norm(act, 1)
            for half in range(2):
                act.wait_ge(sem("z"), half + 1)
                act.activation(half_of(sig, half), bank(half, HALF), ACT.Exp, scale=-1.0).then_inc(sem("ez"), 1)
            act_experts(act, 0)
            for g in range(3):
                act.wait_ge(sem("k0_mm"), g + 1)
                act.activation(kT[:, 0, BANKK * g:BANKK * (g + 1)], bank(g, BANKK), ACT.Copy).then_inc(sem("k0_hi"), 1)
            for g in range(3):
                act.wait_ge(sem("v0_mm"), g + 1)
                act_values(act, 0, g, 3 + g, "v0_out")
            act_norm(act, 2)

            def two_tiles(i):
                for k in range(4):
                    j, half = 2 * i + k // 2, k % 2
                    act.wait_ge(sem("qs_mm"), 4 * i + (k + 1))
                    apart(act, sem("prep"))
                    for s_ in range(2):
                        last = act.activation(qs_part(0, KS_ROWS, j, half, s_),
                                              bank(4 + k, HALF, KS_ROWS).rearrange("p (b q) -> p b q", q=NQ),
                                              ACT.Copy, scale=parity_c[0:KS_ROWS, s_:s_ + 1])
                    last.then_inc(sem("qs_hi"), 1)
            first_loop_last(act, T1 // 2, two_tiles)

            def item(i, n, k):
                b, par, _ = preparation(i, n)
                act.wait_ge(sem("p_mm"), 9 * b + (k + 1))
                if k < 3:
                    act.activation(cT[:, 0, 0, BANKK * k:BANKK * (k + 1)], bank(7, BANKK), ACT.Copy).then_inc(sem("p_hi"), 1)
                elif k < 6:
                    act.activation(kT[:, 0, BANKK * (k - 3):BANKK * (k - 2)], bank(7, BANKK), ACT.Copy).then_inc(sem("p_hi"), 1)
                else:
                    act_values(act, par, k - 6, 7, "p_hi")

            item(-1, 2 * T1 - 2, 0)
            act.wait_ge(sem("b_shT"), 1)
            act.activation(qs[SHIFT_ROW:SHIFT_ROW + 2, 0:R1], shift_rows, ACT.Copy).then_inc(sem("b_sh"), 1)
            item(-1, 2 * T1 - 1, 1)

            def keep_merged(b, kind):
                least(act, sem("om_done"), b - 1)
                act.wait_ge(sem("om_mm"), 2 * b + (kind - 1))
                act.activation(om[:, kind, :], merged(kind), ACT.Copy).then_inc(sem("om_cp"), 1)

            def keep_outputs(tau, n):
                j, par = n % T1, n // T1 % 2
                if isinstance(tau, int) and tau == 0:
                    act.wait_ge(sem("o1_zero"), 1)
                act.wait_ge(sem("b_O"), tau + 1)
                act.activation(o1[64 * (j % 2):64 * (j % 2) + VW, par, j // 2, :], bank(6, R1, VW), ACT.Copy
                               ).then_inc(sem("b_ev"), 1)

            def pair1(i):
                for n in range(2 * T1):
                    tau, j = 2 * T1 * i + n, n % T1
                    if not (isinstance(tau, int) and tau < 2):
                        keep_outputs(tau - 2, (n - 2) % (2 * T1))
                    if j - 1 in MERGE and not (isinstance(i, int) and 2 * i + n // T1 == 0):
                        keep_merged(2 * i + n // T1, MERGE.index(j - 1))
                    for k in preparation(i, n)[2][:-1]:
                        item(i, n, k)
                    for g in range(3):
                        act.wait_ge(sem("b_St"), 3 * tau + (g + 1))
                        part = slice(4 * R1 * g, 4 * R1 * (g + 1))
                        act.activation(p_s[:, n % 2, 0, part], bank(3 + g)[0:KP, 0:4 * R1], ACT.Exp)
                        least(act, sem("b_lo"), 3 * tau + (g - 2))
                        act.activation(p_f[:, part], bank(3 + g)[0:KP, 0:4 * R1], ACT.Exp).then_inc(sem("b_E"), 1)
                    if ahead(i, n, 1):
                        act.wait_ge(sem("b_shT"), tau + 2)
                        apart(act, sem("prep"))
                        act.activation(qs[SHIFT_ROW:SHIFT_ROW + 2, bass.ds(tau * R1 + R1, R1)], shift_rows, ACT.Copy
                                       ).then_inc(sem("b_sh"), 1)
                    for k in preparation(i, n)[2][-1:]:
                        item(i, n, k)
            first_loop_last(act, NB // 2, pair1)
            for tau in (STEPS1 - 2, STEPS1 - 1):
                keep_outputs(tau, tau % (2 * T1))
            for kind in range(2):
                keep_merged(NB, kind)
            act_norm(act, 3)
            act.wait_ge(sem("lg_rel"), 1)
            act.activation(half_of(acc, 0)[:, 0:56], half_of(tmp, 0)[:, 64:120], ACT.Exp).then_inc(sem("lg_exp"), 1)
            act_experts(act, 1)

        @block.vector
        def _(dve):
            chain = [0]

            def link(ins):
                chain[0] += 1
                ins.then_inc(sem("dve_chain"), 1)
                dve.wait_ge(sem("dve_chain"), chain[0])

            def minus(dst, src, hi, scale=None):
                if scale is None:
                    return dve.tensor_tensor(dst, src, hi, ALU.subtract)
                return dve.scalar_tensor_tensor(dst, src, scale, hi, ALU.mult, ALU.subtract)

            def minus_values(parity, g, k):
                v = vals[parity][:, 4 * g:4 * g + 4]
                return minus(v[:, :, :, W1T + 1:VW], bank(k)[0:KP, :].rearrange("p (c j d) -> p c j d", c=4, j=T1), v[:, :, :, 0:W1T])

            def norm(k):
                for h in range(2):
                    dve.wait_ge(sem("n_mean"), 2 * k + h + 1)
                    link(dve.tensor_tensor(half_of(xn, h), half_of(xT, h), bank(h, HALF), ALU.subtract))
                    dve.tensor_tensor(half_of(sq, h), half_of(xn, h), half_of(xn, h), ALU.mult).then_inc(sem("n_sq"), 1)
                for h in range(2):
                    dve.wait_ge(sem("n_sd"), 2 * k + h + 1)
                    link(dve.reciprocal(half_of(sq, h), half_of(sq, h)))
                    if k == 2:
                        link(dve.tensor_tensor(half_of(xn, h), half_of(xn, h), half_of(sq, h), ALU.mult))
                        dve.wait_ge(sem("keep_mm"), 1)
                        dve.tensor_tensor(half_of(xn, h), half_of(xn, h), bank(6, HALF), ALU.mult).then_inc(sem("n_xn"), 1)
                    else:
                        dve.tensor_tensor(half_of(xn, h), half_of(xn, h), half_of(sq, h), ALU.mult).then_inc(sem("n_xn"), 1)
                for h in range(2):
                    dve.wait_ge(sem("n_hi"), 2 * k + h + 1)
                    minus(half_of(xn_s[:, 1, :], h), half_of(xn, h), half_of(xn_s[:, 0, :], h)).then_inc(sem("n_lo"), 1)

            def fold_queries(L):
                def two_heads(i):
                    for k in range(4):
                        h, half = 2 * i + k // 2, k % 2
                        dve.wait_ge(sem(f"q{L}_hi"), 4 * i + (k + 1))
                        dve.scalar_tensor_tensor(dyn_head(1, h, half), bank(4 + k, HALF).rearrange("p (b q) -> p b q", q=NQ),
                                                 qbias[:, bass.ds(h, 1)], dyn_head(0, h, half), ALU.add, ALU.subtract
                                                 ).then_inc(sem(f"q{L}_lo"), 1)
                first_loop_last(dve, H // 2, two_heads)

            def maxima(L, s, n, part):
                if part == 0:
                    dve.wait_ge(sem(f"a{L}_S"), 3 * s + 2)
                    src = ps[:, 0:1024].rearrange("p (j k) -> p j k", k=512)[:, :, 0:BANKK]
                    dve.tensor_reduce(mx[:, 0:1], src, mybir.AxisListType.XY, ALU.max).then_inc(sem(f"a{L}_m"), 1)
                    return
                dve.wait_ge(sem(f"a{L}_S"), 3 * s + 3)
                dve.reduce_max(mx[:, 1:2], bank(2, BANKK), AX).then_inc(sem(f"a{L}_m"), 1)
                if L == 0:
                    dve.wait_ge(sem("a0_m"), 3 * s + 2)
                    dve.tensor_scalar(mx[:, 2:3], mx[:, 0:1], mx[:, 1:2], rcol[:, bass.ds(s, 1)], ALU.max, ALU.add
                                      ).then_inc(sem("a0_m"), 1)
                    dve.wait_ge(sem("a0_m"), 3 * s + 3)
                    dve.tensor_scalar(nb[:, n % 2:n % 2 + 1], mx[:, 2:3], rcol[:, bass.ds(s, 1)], -1.0, ALU.subtract, ALU.mult
                                      ).then_inc(sem("a0_nb"), 1)
                else:
                    dve.wait_ge(sem("a1_m"), 2 * s + 2)
                    dve.tensor_scalar(nb[:, n % 2:n % 2 + 1], mx[:, 0:1], mx[:, 1:2], -1.0, ALU.max, ALU.mult
                                      ).then_inc(sem("a1_nb"), 1)

            def out_lo(L, i, n):
                s = PAIR * i + n
                dve.wait_ge(sem(f"a{L}_ohi"), s)
                b = bank(6 + (n + 1) % 2)
                share = context_share(L, i, n)
                if share:
                    cols_ = slice(share[1], share[1] + 3 * KP)
                    minus(cT[:, share[0], 1, cols_], b[:, 0:3 * KP], cT[:, share[0], 0, cols_]).then_inc(sem(f"cT{L}"), 1)
                minus(qo[:, 1, bass.ds(s * P - P, P)], b[:, 384:512], qo[:, 0, bass.ds(s * P - P, P)]).then_inc(sem(f"a{L}_olo"), 1)

            def attention(L):
                maxima(L, 0, 0, 0)
                maxima(L, 0, 0, 1)

                def pair(i):
                    for n in range(PAIR):
                        s = PAIR * i + n
                        final = isinstance(s, int) and s == STEPS - 1
                        dve.wait_ge(sem(f"a{L}_T"), 3 * s + 1)
                        dve.tensor_copy(pT[:, 0:4 * P], bank(3)[0:KP, :]).then_inc(sem(f"a{L}_pTd"), 1)
                        if not final:
                            maxima(L, s + 1, (n + 1) % PAIR, 0)
                            maxima(L, s + 1, (n + 1) % PAIR, 1)
                        dve.wait_ge(sem(f"a{L}_T"), 3 * s + 3)
                        dve.tensor_copy(pT[:, 8 * P:12 * P], bank(5)[0:KP, :]).then_inc(sem(f"a{L}_pTd"), 1)
                        dve.tensor_reduce(cols[:, n % 2:n % 2 + 1], sums[:, n % 2, :], AX, ALU.add).then_inc(sem(f"a{L}_den"), 1)
                        dve.wait_ge(sem(f"a{L}_den"), s + 1)
                        dve.reciprocal(den[:, n % 2:n % 2 + 1], cols[:, n % 2:n % 2 + 1]).then_inc(sem(f"a{L}_rd"), 1)
                        if not (isinstance(s, int) and s == 0):
                            out_lo(L, i, n)
                first_loop_last(dve, NB // 2, pair)
                dve.wait_ge(sem(f"a{L}_ohi"), STEPS)
                last = slice((STEPS - 1) * P, STEPS * P)
                minus(qo[:, 1, last], bank(6 + (STEPS - 1) % 2)[:, 384:512], qo[:, 0, last]).then_inc(sem(f"a{L}_olo"), 1)

            def residual(L, k):
                for h in range(2):
                    dve.wait_ge(sem(f"proj{L}"), h + 1)
                    if L == 0:
                        link(dve.tensor_scalar(half_of(sq, h), bank(4 + h, HALF), bias_c[:, OB:OB + 1], gates[:, 0:1],
                                               ALU.add, ALU.mult))
                    else:
                        link(dve.tensor_scalar(half_of(sq, h), bank(4 + h, HALF), gates[:, 1:2], None, ALU.mult))
                    dve.tensor_tensor(half_of(xT, h), half_of(xT, h), half_of(sq, h), ALU.add).then_inc(sem(f"x_{k}"), 1)

            def experts(L, round_of=None):
                units = 8 if L == 0 else 4

                def high(e, v):
                    k, de = v % units, v // units
                    if L == 1:
                        dve.wait_ge(sem("f1_silu"), 4 * e + (v + 1))
                        least(dve, sem("f1_lo"), 4 * e + (v - 3))
                        dve.tensor_tensor(hid[:, k % 4, :], bank(2 + k % 2, HALF), sel_silu(k % 2), ALU.mult
                                          ).then_inc(sem("f1_h"), 1)
                    dve.wait_ge(sem(f"f{L}_h"), units * e + (v + 1))
                    least(dve, sem(f"f{L}_Y"), units * e + (v - 3))
                    dve.tensor_copy(hid_s[:, 0, k % 4, :], hid[:, k % 4, :]).then_inc(sem(f"f{L}_hi"), 1)

                def biases(e):
                    dve.wait_ge(sem("f0_h"), 8 * e + 2)
                    dve.tensor_scalar(b1_now[:, :], b1c[:, bass.ds(4 * e, 8)], 0.0, None, ALU.add).then_inc(sem("b1_now"), 1)

                def expert(e):
                    if L == 0 and not (isinstance(e, int) and e == 0):
                        biases(e)
                    for k in range(units):
                        if not (isinstance(e, int) and e == E - 1 and k >= units - 2):
                            high(e, k + 2)
                        if round_of:
                            round_of(e, k)
                if L == 0:
                    dve.tensor_scalar(b1_now[:, :], b1c[:, 0:8], 0.0, None, ALU.add).then_inc(sem("b1_now"), 1)
                high(0, 0)
                high(0, 1)
                first_loop_last(dve, E, expert)

            def tk_round(e, k):
                if k == 0:
                    dve.tensor_tensor(cand[:, :], prefix[:, :], jsh[:, bass.ds(e, 1)], ALU.bitwise_or).then_inc(sem("tk"), 1)
                if k == 1:
                    dve.wait_ge(sem("tk"), 5 * e + 1)
                    dve.tensor_scalar(tmp, sig, cand[:, :].bitcast(F32), 0.0, ALU.is_ge, ALU.add, accum_out=flag[:, 1:2]
                                      ).then_inc(sem("tk"), 1)
                if k == 2:
                    dve.wait_ge(sem("tk"), 5 * e + 2)
                    dve.tensor_scalar(flag[:, 0:1], flag[:, 1:2], float(TOPK), valid[:, bass.ds(e, 1)], ALU.is_ge, ALU.mult
                                      ).then_inc(sem("tk_flag"), 1)
                if k == 5:
                    dve.wait_ge(sem("tk_sum"), e + 1)
                    dve.tensor_scalar(digit[:, 0:1], bank(0, 1), -1.0, powc[:, bass.ds(e, 1)], ALU.add, ALU.mult
                                      ).then_inc(sem("tk"), 1)
                if k == 6:
                    dve.wait_ge(sem("tk"), 5 * e + 3)
                    dve.tensor_copy(digit_i[:, :], digit[:, 0:1]).then_inc(sem("tk"), 1)
                if k == 7:
                    dve.wait_ge(sem("tk"), 5 * e + 4)
                    dve.tensor_tensor(prefix[:, :], prefix[:, :], digit_i[:, :], ALU.bitwise_or).then_inc(sem("tk"), 1)
                    dve.wait_ge(sem("tk"), 5 * e + 5)

            def combine(L, k):
                for e in range(E):
                    for h in range(2):
                        dve.wait_ge(sem(f"gb{L}"), 2 * e + h + 1)
                        dve.wait_ge(sem(f"f{L}_y"), 2 * E)
                        y = y_e[:, e * TOK + HALF * h:e * TOK + HALF * (h + 1)]
                        if e == 0:
                            dve.tensor_tensor(half_of(acc, h), y, bank(h, HALF), ALU.mult).then_inc(sem(f"c{L}"), 1)
                            dve.wait_ge(sem(f"c{L}"), 2 * e + h + 1)
                        else:
                            dve.tensor_tensor(y, y, bank(h, HALF), ALU.mult).then_inc(sem(f"c{L}"), 1)
                            dve.wait_ge(sem(f"c{L}"), 2 * e + h + 1)
                            link(dve.tensor_tensor(half_of(acc, h), half_of(acc, h), y, ALU.add))
                for h in range(2):
                    dve.scalar_tensor_tensor(half_of(xT, h), half_of(acc, h), gates[:, 2 + L:3 + L], half_of(xT, h),
                                             ALU.mult, ALU.add).then_inc(sem(f"x_{k}"), 1)

            for k, (load, srcs, rows, f32, split, col) in enumerate(groups):
                if split is None:
                    continue
                dve.wait_ge(sem("prep_a"), k + 1)
                n = rows * len(srcs)
                minus(split[:, 1, col:col + n], bank(k % 8, n), split[:, 0, col:col + n]).then_inc(sem("prep_d"), 1)
            for g in range(8):
                dve.wait_ge(sem("fold_hi"), g + 1)
                dst, scale = (Ms, DH0 ** -0.5) if g < 4 else (Ns, 1.0)
                last = minus(fold_part(dst, 1, g), bank(g).rearrange("p (c n) -> p c n", n=C), fold_part(dst, 0, g), scale)
                last.then_inc(sem("M0" if g < 4 else "N0"), 1)
                if g == 3:
                    dve.wait_ge(sem("ld_small"), 160)
                    dve.wait_ge(sem("consts"), 1)
                    for s_ in range(2):
                        r = slice(64 * s_, 64 * s_ + 64)
                        dve.tensor_tensor(prod[r, s_:H:2], bias_c[r, BQ:BQ + 8], bias_c[r, BK:BK + 8], ALU.mult).then_inc(sem("prod"), 1)
            dve.wait_ge(sem("bias_mm"), 1)
            SC = DH0 ** -0.5
            for s_ in range(2):
                dve.tensor_scalar(qbias[:, s_:H:2], bank(s_)[:, s_:H:2], SC, None, ALU.mult)
                dve.tensor_scalar(U[:, s_:H:2], bank(s_)[:, 16 + s_:32:2], SC, None, ALU.mult)
            dve.tensor_scalar(crow[:, :], bank(0)[0:H, 33:34], SC, None, ALU.mult)
            link(dve.tensor_tensor(bias_c[:, OB:OB + 1], bank(0)[:, 32:33], bias_c[:, BO:BO + 1], ALU.add))
            for r, sh in enumerate(SHIFTS):
                last = dve.tensor_scalar(jsh[:, r:r + 1], pj[:, r:r + 1], 15, sh, ALU.bitwise_and, ALU.logical_shift_left)
            link(last)
            link(dve.tensor_copy(cols[:, 7:8], jsh[:, 7:8]))
            link(dve.tensor_scalar(valid[:, 7:8], cols[:, 7:8], 8.0, None, ALU.is_lt))
            link(dve.tensor_scalar(prefix[:, :], jsh[:, 0:1], 0, None, ALU.bitwise_and))
            dve.tensor_copy(Wg_rep[:, :, :], wg_raw[:, :].unsqueeze(2).broadcast_to([P, E, 16])).then_inc(sem("bias_cols"), 1)
            dve.wait_ge(sem("N0"), 4)
            dve.wait_ge(sem("M0"), 4)
            dve.sem_inc(sem("folds0"), 8)

            norm(0)
            fold_queries(0)
            dve.wait_ge(sem("r_T"), 1)
            dve.tensor_copy(rcol[:, :], bank(0)[:, 0:STEPS]).then_inc(sem("rcol"), 1)
            dve.wait_ge(sem("rcol"), 1)
            attention(0)
            dve.wait_ge(sem("tanh"), 1)
            residual(0, 1)
            norm(1)
            for h in range(2):
                dve.wait_ge(sem("ez"), h + 1)
                link(dve.tensor_scalar(half_of(sig, h), half_of(sig, h), 1.0, None, ALU.add))
                link(dve.reciprocal(half_of(sig, h), half_of(sig, h)))
            experts(0, tk_round)
            thr = prefix[:, :].bitcast(F32)
            link(dve.tensor_scalar(sel, sig, thr, 0.0, ALU.is_gt, ALU.add, accum_out=flag[:, 1:2]))
            link(dve.tensor_scalar(flag[:, 0:1], flag[:, 1:2], -1.0, float(TOPK), ALU.mult, ALU.add))
            link(dve.tensor_scalar(tmp, sig, thr, None, ALU.is_equal))
            link(dve.memset(sq[:, :], 1.0))
            link(dve.tensor_tensor_scan(acc, tmp, sq[:, :], 0.0, ALU.add, ALU.mult))
            link(dve.tensor_scalar(acc, acc, flag[:, 0:1], None, ALU.is_le))
            link(dve.tensor_tensor(tmp, tmp, acc, ALU.mult))
            link(dve.tensor_tensor(sel, sel, tmp, ALU.add))
            dve.tensor_tensor(sel, sel, sig, ALU.mult).then_inc(sem("g0"), 1)
            combine(0, 2)
            dve.wait_ge(sem("ld_mask"), 16)
            dve.tensor_scalar(mbias[:, :].rearrange("q (c p) -> q c p", p=KP), mask_i.rearrange("q (p c) -> q c p", c=KC),
                              0.0, MASKED, ALU.is_equal, ALU.mult).then_inc(sem("mbias"), 1)
            dve.wait_ge(sem("mbias"), 1)
            link(dve.reduce_max(keep[:, 0:1], mbias[:, :], AX))
            link(dve.tensor_scalar(keep[:, 1:2], keep[:, 0:1], 0.0, None, ALU.is_ge))
            dve.tensor_scalar(repk[:, :], rep[:, :], keep[:, 1:2], None, ALU.mult).then_inc(sem("repk"), 1)
            for a in range(2):
                last = dve.memset(vals[a][:, :, :, W1T:W1T + 1], 1.0)
            last.then_inc(sem("v_ones"), 1)
            for g in range(3):
                dve.wait_ge(sem("k0_hi"), g + 1)
                c_ = slice(BANKK * g, BANKK * (g + 1))
                minus(kT[:, 1, c_], bank(g, BANKK), kT[:, 0, c_]).then_inc(sem("k0_lo"), 1)
            for g in range(3):
                dve.wait_ge(sem("v0_out"), g + 1)
                minus_values(0, g, 3 + g).then_inc(sem("v0_lo"), 1)
            norm(2)
            dve.memset(sq[:, :], 0.0).then_inc(sem("o1_zero"), 1)

            def two_tiles(i):
                for k in range(4):
                    j, half = 2 * i + k // 2, k % 2
                    dve.wait_ge(sem("qs_hi"), 4 * i + (k + 1))
                    lo = slice(STACK[1], STACK[1] + W1T)
                    for s_ in range(2):
                        dst = qs_part(lo.start, lo.stop, j, half, s_)
                        last = dve.scalar_tensor_tensor(dst, bank(4 + k, HALF)[lo].rearrange("p (b q) -> p b q", q=NQ),
                                                        parity_c[lo, s_:s_ + 1], dst, ALU.mult, ALU.subtract)
                    last.then_inc(sem("qs_lo"), 1)
            first_loop_last(dve, T1 // 2, two_tiles)

            def maxima1(tau, n):
                dve.wait_ge(sem("b_Sq"), 2 * tau + 1)
                dve.tensor_reduce(mx[0:R1, 0:1], ps[0:R1, 0:1024].rearrange("p (j k) -> p j k", k=512)[:, :, 0:BANKK],
                                  mybir.AxisListType.XY, ALU.max)
                dve.wait_ge(sem("b_Sq"), 2 * tau + 2)
                dve.reduce_max(mx[0:R1, 1:2], bank(2, BANKK, R1), AX).then_inc(sem("b_m"), 1)
                dve.wait_ge(sem("b_m"), tau + 1)
                dve.tensor_scalar(mx[0:R1, 2:3], mx[0:R1, 0:1], mx[0:R1, 1:2], -1.0, ALU.max, ALU.mult).then_inc(sem("b_c"), 1)
                dve.wait_ge(sem("b_c"), 2 * tau + 1)
                dve.tensor_copy(mh[:, n % 2, 0:1], mx[0:R1, 2:3]).then_inc(sem("b_c"), 1)
                dve.wait_ge(sem("b_c"), 2 * tau + 2)
                dve.tensor_tensor(mh[:, n % 2, 1:2], mx[0:R1, 2:3], mh[:, n % 2, 0:1], ALU.subtract).then_inc(sem("b_h"), 1)

            def item(i, n, k):
                b, par, _ = preparation(i, n)
                dve.wait_ge(sem("p_hi"), 9 * b + (k + 1))
                c_ = slice(BANKK * (k % 3), BANKK * (k % 3 + 1))
                hi, lo = (cT[:, 0, 0, c_], cT[:, 0, 1, c_]) if k < 3 else (kT[:, 0, c_], kT[:, 1, c_])
                if k < 6:
                    last = minus(lo, bank(7, BANKK), hi)
                else:
                    last = minus_values(par, k - 6, 7)
                last.then_inc(sem("p_lo"), 1)

            def scale_outputs(b):
                dve.wait_ge(sem("om_cp"), 2 * b)
                dve.reciprocal(om[:, 1, :], om[:, 1, :]).then_inc(sem("rsum"), 1)
                dve.wait_ge(sem("rsum"), b)
                dve.tensor_tensor(aT[:, bass.ds(NQ * b - NQ, NQ)], om[:, 0, :], om[:, 1, :], ALU.mult).then_inc(sem("om_done"), 1)

            maxima1(0, 0)
            item(-1, 2 * T1 - 2, 0)
            maxima1(1, 1)
            item(-1, 2 * T1 - 1, 1)

            def pair1(i):
                for n in range(2 * T1):
                    tau, j, b = 2 * T1 * i + n, n % T1, 2 * i + n // T1
                    if ahead(i, n, 2):
                        maxima1(tau + 2, n)
                    for k in preparation(i, n)[2]:
                        item(i, n, k)
                    if j == MERGE[1] + 1 and not (isinstance(b, int) and b == 0):
                        scale_outputs(b)
            first_loop_last(dve, NB // 2, pair1)
            scale_outputs(NB)
            residual(1, 3)
            norm(3)
            T7 = 7
            lg = tmp[:, 0:56]
            rel = tmp[:, 64:120]
            ex = acc[:, 0:56]
            v3 = lambda a: a.rearrange("p (t e) -> p t e", e=E)
            gt = sig[:, 0:448].rearrange("p (t e j) -> p t e j", t=T7, e=E)
            eq = sig[:, 448:896].rearrange("p (t e j) -> p t e j", t=T7, e=E)
            dve.wait_ge(sem("lg"), 1)
            link(dve.tensor_copy(lg, bank(0)[:, 0:56]))
            lj = v3(lg).unsqueeze(2).broadcast_to([P, T7, E, E])
            le = v3(lg).unsqueeze(3).broadcast_to([P, T7, E, E])
            link(dve.tensor_tensor(gt, lj, le, ALU.is_gt))
            link(dve.tensor_tensor(eq, lj, le, ALU.is_equal))
            link(dve.tensor_tensor(eq, eq, tril[:, :, :].unsqueeze(1).broadcast_to([P, T7, E, E]), ALU.mult))
            link(dve.tensor_tensor(gt, gt, eq, ALU.add))
            rank = sel[:, 0:56]
            link(dve.tensor_reduce(rank, gt.rearrange("p t e j -> p (t e) j"), AX, ALU.add))
            link(dve.tensor_scalar(rank, rank, 2.0, None, ALU.is_lt))
            top = sel[:, 64:71]
            link(dve.tensor_reduce(top, v3(lg), AX, ALU.max))
            dve.tensor_tensor(v3(rel), v3(lg), top.unsqueeze(2).broadcast_to([P, T7, E]), ALU.subtract).then_inc(sem("lg_rel"), 1)
            dve.wait_ge(sem("lg_exp"), 1)
            link(dve.tensor_tensor(ex, ex, rank, ALU.mult))
            link(dve.tensor_reduce(top, v3(ex), AX, ALU.add))
            link(dve.reciprocal(top, top))
            dve.tensor_tensor(v3(lg), v3(ex), top.unsqueeze(2).broadcast_to([P, T7, E]), ALU.mult).then_inc(sem("rw"), 1)
            dve.wait_ge(sem("rw_T"), 1)
            link(dve.tensor_copy(sel[0:E, 0:512], bank(0)[0:E, :]))
            dve.tensor_copy(sel[0:E, 512:896], bank(1)[0:E, 0:384]).then_inc(sem("g1"), 1)
            experts(1)
            combine(1, 4)
            for g in range(2):
                dve.wait_ge(sem("xT_rows"), g + 1)
                n = 512 if g == 0 else 384
                dve.tensor_copy(xn[:, 512 * g:512 * g + n], bank(g, n)).then_inc(sem("out_rows"), 1)


_INS = ['x', 'ctx_1024', 'mask_1x1xSxS2_ik0', 'g_xattn', 'g_ffn', 'L0_xattn_Wq', 'L0_xattn_bq', 'L0_xattn_Wk',
        'L0_xattn_bk', 'L0_xattn_Wv', 'L0_xattn_bv', 'L0_xattn_Wo', 'L0_xattn_bo', 'L0_ffn_Wg', 'L0_ffn_W1',
        'L0_ffn_b1', 'L0_ffn_W2', 'L0_ffn_b2', 'L1_xattn_w_q', 'L1_xattn_w_k', 'L1_xattn_w_v', 'L1_xattn_w_o',
        'L1_ffn_Wr', 'L1_ffn_W1', 'L1_ffn_W2']


def kernel(**inputs):
    import numpy as _np
    import concourse.bacc as _bacc
    from concourse import mybir as _mybir
    from concourse.bass_utils import run_bass_kernel_spmd as _run

    nc = _bacc.Bacc("TRN2", target_bir_lowering=False, num_devices=1)
    arrays, args = {}, []
    for name in _INS:
        a = _np.ascontiguousarray(inputs[name])
        arrays[f"in_{name}_dram"] = a
        args.append(nc.dram_tensor(f"in_{name}_dram", a.shape, _mybir.dt.from_np(a.dtype), kind="ExternalInput").ap())
    args.append(nc.dram_tensor("out_0_dram", (NB, NQ, C), F32, kind="ExternalOutput").ap())
    flamingo(nc, *args)
    r = _run(nc, [arrays], core_ids=[0])
    return r.results[0]["out_0_dram"]
```
